# Optimizing a Trainium2 kernel written in Bass

```python
import numpy as np
import jax
import jax.numpy as jnp

def _softmax(x, axis=-1):
    return jax.nn.softmax(x, axis=axis)

def _gelu(x):
    return jax.nn.gelu(x, approximate=True)

def _silu(x):
    return jax.nn.silu(x)

def _sigmoid(x):
    return jax.nn.sigmoid(x)

def _layernorm(x, axis=-1, eps=1e-05):
    m = jnp.mean(x, axis=axis, keepdims=True)
    v = jnp.var(x, axis=axis, keepdims=True)
    return (x - m) / jnp.sqrt(v + eps)

def _scatter_add(tgt, idx, src, axis=0):
    return tgt.at[idx].add(src)

def _segment_sum(src, seg, n):
    return jax.ops.segment_sum(src, seg, n)
kernel_name = 'mk_gps_d1_gnn_r8_305a37'

def setup_inputs(seed: int=0):
    np.random.seed(seed)
    _w = jnp.asarray

    def _rec_inputs():
        import jax
        import jax.numpy as jnp
        _gk = jax.random.key(seed)
        x = -0.0003713 + 1 * jax.random.normal(jax.random.fold_in(_gk, 1), (12500, 256), jnp.float32)
        src = jax.random.randint(jax.random.fold_in(_gk, 2), (200000,), 0, 12500, jnp.int32)
        dst = jnp.minimum((12500 * jax.random.uniform(jax.random.fold_in(_gk, 3), (200000,)) ** 2.0).astype(jnp.int32), 99999)
        _o = jnp.argsort(dst, stable=True)
        src = src[_o]
        dst = dst[_o]
        return (x, src, dst)
    x, src, dst = _rec_inputs()

    def _L0_gnn_setup():
        import jax, jax.numpy as jnp
        import numpy as np
        N, IN_CH, HEADS, OUT_CH, E = (6250, 256, 4, 64, 100000)
        key = jax.random.key(seed)
        k1, k2, k3, k4, k5 = jax.random.split(key, 5)
        x = jax.random.normal(k1, (N, IN_CH), dtype=jnp.float32)
        edge_index = jax.random.randint(k2, (2, E), 0, N, dtype=jnp.int64)
        bw = float(np.sqrt(6.0 / (IN_CH + HEADS * OUT_CH)))
        ba = float(np.sqrt(6.0 / (HEADS + OUT_CH)))
        weight = jax.random.uniform(k3, (IN_CH, HEADS * OUT_CH), jnp.float32, -bw, bw)
        attn_l = jax.random.uniform(k4, (HEADS, OUT_CH), jnp.float32, -ba, ba)
        attn_r = jax.random.uniform(k5, (HEADS, OUT_CH), jnp.float32, -ba, ba)
        return {'x': x, 'edge_index': edge_index, 'weight': weight, 'attn_l': attn_l, 'attn_r': attn_r}
    _L0_gnn_all = _L0_gnn_setup()
    _L0_gnn_in = {k: v for k, v in _L0_gnn_all.items() if k in ('weight', 'attn_l', 'attn_r')}
    del _L0_gnn_all

    def _L0_mix_setup():
        import jax, jax.numpy as jnp
        import numpy as np
        NHEAD = 8
        ATT_EPS = 1e-06
        LN_EPS = 1e-05

        def _layernorm(x, g, b):
            mu = jnp.mean(x, axis=-1, keepdims=True)
            var = jnp.mean(jnp.square(x - mu), axis=-1, keepdims=True)
            return (x - mu) * jax.lax.rsqrt(var + LN_EPS) * g + b
        key = jax.random.key(seed)
        ks = jax.random.split(key, 7)
        N, L, C = (4, 2048, 256)
        s = 1.0 / np.sqrt(C)
        return {'x': jax.random.normal(ks[0], (N, L, C), jnp.float32), 'Wq': jax.random.normal(ks[1], (C, C), jnp.float32) * s, 'Wk': jax.random.normal(ks[2], (C, C), jnp.float32) * s, 'Wv': jax.random.normal(ks[3], (C, C), jnp.float32) * s, 'Wm': jax.random.normal(ks[4], (C, C), jnp.float32) * s, 'W1': jax.random.normal(ks[5], (2 * C, 2 * C), jnp.float32) * (1.0 / np.sqrt(2 * C)), 'W2': jax.random.normal(ks[6], (2 * C, C), jnp.float32) * (1.0 / np.sqrt(2 * C)), 'g1': jnp.ones((C,), jnp.float32), 'b1': jnp.zeros((C,), jnp.float32), 'g2': jnp.ones((C,), jnp.float32), 'b2': jnp.zeros((C,), jnp.float32)}
    _L0_mix_all = _L0_mix_setup()
    _L0_mix_in = {k: v for k, v in _L0_mix_all.items() if k in ('Wq', 'Wk', 'Wv', 'Wm', 'W1', 'W2', 'g1', 'b1', 'g2', 'b2')}
    del _L0_mix_all

    def _L0_ffn_setup():
        import jax, jax.numpy as jnp
        import numpy as np
        B, A = (512, 8)
        IN, OUT = (256, 256)
        SH1, SH2 = (256, 128)
        EH1, EH2 = (128, 64)
        E, TOPK = (4, 2)

        def _shared_mlp(x, W1, b1, W2, b2, W3, b3):
            h = jax.nn.relu(x @ W1 + b1)
            h = jax.nn.relu(h @ W2 + b2)
            return h @ W3 + b3

        def _experts_mlp(x, eW1, eb1, eW2, eb2, eW3, eb3):
            h = jax.nn.relu(jnp.einsum('baf,efh->ebah', x, eW1) + eb1[:, None, None, :])
            h = jax.nn.relu(jnp.einsum('ebah,ehg->ebag', h, eW2) + eb2[:, None, None, :])
            o = jnp.einsum('ebag,ego->ebao', h, eW3) + eb3[:, None, None, :]
            return jnp.moveaxis(o, 0, -1)
        key = jax.random.key(seed)
        ks = jax.random.split(key, 16)
        s = 0.05
        return {'x': jax.random.normal(ks[0], (B, A, IN), jnp.float32), 'sW1': jax.random.normal(ks[1], (IN, SH1), jnp.float32) * s, 'sb1': jnp.zeros((SH1,), jnp.float32), 'sW2': jax.random.normal(ks[2], (SH1, SH2), jnp.float32) * s, 'sb2': jnp.zeros((SH2,), jnp.float32), 'sW3': jax.random.normal(ks[3], (SH2, OUT), jnp.float32) * s, 'sb3': jnp.zeros((OUT,), jnp.float32), 'eW1': jax.random.normal(ks[4], (E, IN, EH1), jnp.float32) * s, 'eb1': jnp.zeros((E, EH1), jnp.float32), 'eW2': jax.random.normal(ks[5], (E, EH1, EH2), jnp.float32) * s, 'eb2': jnp.zeros((E, EH2), jnp.float32), 'eW3': jax.random.normal(ks[6], (E, EH2, OUT), jnp.float32) * s, 'eb3': jnp.zeros((E, OUT), jnp.float32), 'gW': jax.random.normal(ks[7], (IN, E), jnp.float32) * s, 'gb': jnp.zeros((E,), jnp.float32)}
    _L0_ffn_all = _L0_ffn_setup()
    _L0_ffn_in = {k: v for k, v in _L0_ffn_all.items() if k in ('sW1', 'sb1', 'sW2', 'sb2', 'sW3', 'sb3', 'eW1', 'eb1', 'eW2', 'eb2', 'eW3', 'eb3', 'gW', 'gb')}
    del _L0_ffn_all
    return {'x': x, 'src': src, 'dst': dst, 'L0_gnn_weight': _L0_gnn_in['weight'], 'L0_gnn_attn_l': _L0_gnn_in['attn_l'], 'L0_gnn_attn_r': _L0_gnn_in['attn_r'], 'L0_mix_Wq': _L0_mix_in['Wq'], 'L0_mix_Wk': _L0_mix_in['Wk'], 'L0_mix_Wv': _L0_mix_in['Wv'], 'L0_mix_Wm': _L0_mix_in['Wm'], 'L0_mix_W1': _L0_mix_in['W1'], 'L0_mix_W2': _L0_mix_in['W2'], 'L0_mix_g1': _L0_mix_in['g1'], 'L0_mix_b1': _L0_mix_in['b1'], 'L0_mix_g2': _L0_mix_in['g2'], 'L0_mix_b2': _L0_mix_in['b2'], 'L0_ffn_sW1': _L0_ffn_in['sW1'], 'L0_ffn_sb1': _L0_ffn_in['sb1'], 'L0_ffn_sW2': _L0_ffn_in['sW2'], 'L0_ffn_sb2': _L0_ffn_in['sb2'], 'L0_ffn_sW3': _L0_ffn_in['sW3'], 'L0_ffn_sb3': _L0_ffn_in['sb3'], 'L0_ffn_eW1': _L0_ffn_in['eW1'], 'L0_ffn_eb1': _L0_ffn_in['eb1'], 'L0_ffn_eW2': _L0_ffn_in['eW2'], 'L0_ffn_eb2': _L0_ffn_in['eb2'], 'L0_ffn_eW3': _L0_ffn_in['eW3'], 'L0_ffn_eb3': _L0_ffn_in['eb3'], 'L0_ffn_gW': _L0_ffn_in['gW'], 'L0_ffn_gb': _L0_ffn_in['gb']}

def reference(x, src, dst, L0_gnn_weight, L0_gnn_attn_l, L0_gnn_attn_r, L0_mix_Wq, L0_mix_Wk, L0_mix_Wv, L0_mix_Wm, L0_mix_W1, L0_mix_W2, L0_mix_g1, L0_mix_b1, L0_mix_g2, L0_mix_b2, L0_ffn_sW1, L0_ffn_sb1, L0_ffn_sW2, L0_ffn_sb2, L0_ffn_sW3, L0_ffn_sb3, L0_ffn_eW1, L0_ffn_eb1, L0_ffn_eW2, L0_ffn_eb2, L0_ffn_eW3, L0_ffn_eb3, L0_ffn_gW, L0_ffn_gb):
    import jax
    import jax.numpy as jnp

    def _L0_gnn_ref(x, edge_index, weight, attn_l, attn_r):
        import jax, jax.numpy as jnp
        import numpy as np
        N, IN_CH, HEADS, OUT_CH, E = (6250, 256, 4, 64, 100000)
        heads, out_ch = attn_l.shape
        n = x.shape[0]
        xt = jnp.matmul(x, weight).reshape(-1, heads, out_ch)
        row, col = (edge_index[0], edge_index[1])
        alpha_l = jnp.einsum('ehd,hd->eh', xt[row], attn_l)
        alpha_r = jnp.einsum('ehd,hd->eh', xt[col], attn_r)
        alpha = jax.nn.softmax(jax.nn.leaky_relu(alpha_l + alpha_r, 0.01), axis=1)
        tmp = jnp.einsum('nh,nhd->nd', alpha[:n], xt[col[:n]])
        out = jnp.broadcast_to(tmp[:, None, :], (n, heads, out_ch))
        return out.reshape(n, heads * out_ch)

    def _L0_mix_ref(x, Wq, Wk, Wv, Wm, W1, W2, g1, b1, g2, b2):
        import jax, jax.numpy as jnp
        import numpy as np
        NHEAD = 8
        ATT_EPS = 1e-06
        LN_EPS = 1e-05

        def _layernorm(x, g, b):
            mu = jnp.mean(x, axis=-1, keepdims=True)
            var = jnp.mean(jnp.square(x - mu), axis=-1, keepdims=True)
            return (x - mu) * jax.lax.rsqrt(var + LN_EPS) * g + b
        N, L, C = x.shape
        H = NHEAD
        D = C // H
        q = (x @ Wq).reshape(N, L, H, D)
        k = (x @ Wk).reshape(N, L, H, D)
        v = (x @ Wv).reshape(N, L, H, D)
        Q = jax.nn.elu(q) + 1.0
        K = jax.nn.elu(k) + 1.0
        v = v / L
        KV = jnp.einsum('nshd,nshv->nhdv', K, v)
        Z = 1.0 / (jnp.einsum('nlhd,nhd->nlh', Q, K.sum(axis=1)) + ATT_EPS)
        msg = jnp.einsum('nlhd,nhdv,nlh->nlhv', Q, KV, Z) * L
        msg = msg.reshape(N, L, C) @ Wm
        msg = _layernorm(msg, g1, b1)
        h = jnp.concatenate([x, msg], axis=-1) @ W1
        h = jax.nn.relu(h) @ W2
        msg = _layernorm(h, g2, b2)
        return x + msg

    def _L0_ffn_ref(x, sW1, sb1, sW2, sb2, sW3, sb3, eW1, eb1, eW2, eb2, eW3, eb3, gW, gb):
        import jax, jax.numpy as jnp
        import numpy as np
        B, A = (512, 8)
        IN, OUT = (256, 256)
        SH1, SH2 = (256, 128)
        EH1, EH2 = (128, 64)
        E, TOPK = (4, 2)

        def _shared_mlp(x, W1, b1, W2, b2, W3, b3):
            h = jax.nn.relu(x @ W1 + b1)
            h = jax.nn.relu(h @ W2 + b2)
            return h @ W3 + b3

        def _experts_mlp(x, eW1, eb1, eW2, eb2, eW3, eb3):
            h = jax.nn.relu(jnp.einsum('baf,efh->ebah', x, eW1) + eb1[:, None, None, :])
            h = jax.nn.relu(jnp.einsum('ebah,ehg->ebag', h, eW2) + eb2[:, None, None, :])
            o = jnp.einsum('ebag,ego->ebao', h, eW3) + eb3[:, None, None, :]
            return jnp.moveaxis(o, 0, -1)
        all_out = _experts_mlp(x, eW1, eb1, eW2, eb2, eW3, eb3)
        shared = _shared_mlp(x, sW1, sb1, sW2, sb2, sW3, sb3)
        gates = jax.nn.softmax(x @ gW + gb, axis=-1)
        topv, topi = jax.lax.top_k(gates, TOPK)
        topw = jax.nn.softmax(topv, axis=-1)
        sel = jnp.take_along_axis(all_out, topi[:, :, None, :], axis=-1)
        gated = jnp.sum(sel * topw[:, :, None, :], axis=-1)
        return shared + gated
    edge_index = jnp.stack([src, dst])
    xn = _layernorm(x, axis=-1)
    x = x + _L0_gnn_ref(xn, edge_index, L0_gnn_weight, L0_gnn_attn_l, L0_gnn_attn_r) + _L0_mix_ref(xn[None], L0_mix_Wq, L0_mix_Wk, L0_mix_Wv, L0_mix_Wm, L0_mix_W1, L0_mix_W2, L0_mix_g1, L0_mix_b1, L0_mix_g2, L0_mix_b2)[0]
    x = x + _L0_ffn_ref(_layernorm(x, axis=-1)[None], L0_ffn_sW1, L0_ffn_sb1, L0_ffn_sW2, L0_ffn_sb2, L0_ffn_sW3, L0_ffn_sb3, L0_ffn_eW1, L0_ffn_eb1, L0_ffn_eW2, L0_ffn_eb2, L0_ffn_eW3, L0_ffn_eb3, L0_ffn_gW, L0_ffn_gb)[0]
    return x

_drawn_inputs = setup_inputs


def setup_inputs(seed=0):
    import zlib

    import numpy as np

    out = dict(_drawn_inputs(seed))
    spreads = {'L0_mix_g1': (1.0, 0.2),
     'L0_mix_b1': (0.0, 0.1),
     'L0_mix_g2': (1.0, 0.2),
     'L0_mix_b2': (0.0, 0.1),
     'L0_ffn_sb1': (0.0, 0.8),
     'L0_ffn_sb2': (0.0, 0.445),
     'L0_ffn_sb3': (0.0, 0.1),
     'L0_ffn_eb1': (0.0, 0.8),
     'L0_ffn_eb2': (0.0, 0.8),
     'L0_ffn_eb3': (0.0, 0.286),
     'L0_ffn_gb': (0.0, 0.8)}
    factors = {'L0_ffn_eW1': 3.066, 'L0_ffn_eW2': 2.679}
    for name, (base, spread) in spreads.items():
        noise = np.random.default_rng([zlib.crc32(name.encode()), seed]).standard_normal(out[name].shape)
        drawn = base * np.exp(spread * noise) if base else spread * noise
        out[name] = jnp.asarray(drawn.astype(out[name].dtype))
    for name, factor in factors.items():
        out[name] = (out[name] * factor).astype(out[name].dtype)
    return out
```

```python
from contextlib import ExitStack

import concourse.bass as bass
from concourse import mybir

F32 = mybir.dt.float32
F32R = mybir.dt.float32r
I32 = mybir.dt.int32
ALU = mybir.AluOpType
ACT = mybir.ActivationFunctionType
AXX = mybir.AxisListType.X

N_NODES = 12500
C = 256
HEADS, HEAD_CH = 4, 64
MIX_HEADS, MIX_CH = 8, 32
EXPERTS, TOPK = 4, 2
LN_EPS, ATT_EPS = 1e-5, 1e-6

P = 128
R = 125
T = 4
GR = R * T
NG = N_NODES // GR
CK = C // P
BANK = 512
XT_W = C + HEADS
XA_W = XT_W + HEADS
KX_W = C + 2

W_AT, W_TOTAL = {}, 0
for _name, _chunks, _cols in (("Wq", 2, 256), ("W1", 4, 512), ("W2", 4, 256), ("sW1", 2, 256), ("sW2", 2, 128),
                              ("sW3", 1, 256), ("eW1", 8, 128), ("eW2", 4, 128), ("eW3", 2, 256)):
    W_AT[_name] = (W_TOTAL, _cols)
    W_TOTAL += _chunks * _cols


def gps_layer(nc, A):
    ctx = ExitStack()
    with ctx:
        def sb(name, shape, dt=F32, stack=ctx):
            return stack.enter_context(nc.sbuf_tensor(name, shape, dt))

        sems = {}

        def sem(name):
            if name not in sems:
                sems[name] = ctx.enter_context(nc.semaphore("s_" + name))
            return sems[name]

        def need(eng, name, count):
            if not (isinstance(count, int) and count <= 0):
                eng.wait_ge(sem(name), count)

        table_xt = nc.dram_tensor("table_xt", [N_NODES, XT_W], F32)
        table_al = nc.dram_tensor("table_al", [N_NODES, HEADS], F32)
        xt_rows = table_xt.ap().rearrange("(g p j) n -> g p j n", p=R, j=T)
        al_rows = table_al.ap().rearrange("(g p j) n -> g p j n", p=R, j=T)
        x_rows = A["x"].rearrange("(g p j) n -> g p j n", p=R, j=T)
        out_rows = A["out"].rearrange("(g p j) n -> g p j n", p=R, j=T)
        src_rows = A["src"][0:N_NODES].rearrange("(g p j) -> g p j", p=R, j=T)
        dst_rows = A["dst"][0:N_NODES].rearrange("(g p j) -> g p j", p=R, j=T)

        ident = sb("ident", [P, P])
        w_hi = sb("w_hi", [P, W_TOTAL], F32R)
        w_lo = sb("w_lo", [P, W_TOTAL], F32R)
        gate_w = sb("gate_w", [P, CK, P], F32R)
        out_bias = sb("out_bias", [P, C], F32R)
        gate_sel = sb("gate_sel", [P, 2, P], F32R)
        ksum_h = sb("ksum_h", [P, CK, MIX_HEADS])
        den_sel = sb("den_sel", [P, CK, P], F32R)
        den_rows = sb("den_rows", [R, T, P])
        g_hi = sb("g_hi", [P, CK, C], F32R)
        g_lo = sb("g_lo", [P, CK, C], F32R)
        g2_bc = sb("g2_bc", [R, C])
        b2_bc = sb("b2_bc", [R, C])
        h_bias = sb("h_bias", [P, 4])
        s1_bias = sb("s1_bias", [P, 2])
        e1_bias = sb("e1_bias", [P, EXPERTS])
        s2_bias = sb("s2_bias", [P, 1])
        e2_bias = sb("e2_bias", [P, 2])
        gate_bias = sb("gate_bias", [P, 1])
        beats = sb("beats", [R, EXPERTS, 2, EXPERTS])
        neg_half = sb("neg_half", [R, T])
        eps = sb("eps", [R, T])
        gate_rows = sb("gate_rows", [R, T, P])
        rs1 = sb("rs1", [R, T])
        xb = [sb(f"xb{n}", [R, T, C]) for n in range(2)]
        bn = sb("bn", [R, T, 6])
        mv = [sb(f"mv_{n}", [R, T, 2]) for n in "xmyz"]
        rs = [sb(f"rs_{n}", [R, T]) for n in "xmyz"]
        nm = [sb(f"nm_{n}", [R, T]) for n in "xmyz"]
        veps = [sb(f"veps_{n}", [R, T]) for n in "xmyz"]
        nmean = [sb(f"nmean_{n}", [R, T]) for n in "xmyz"]
        LX, LM, LY, LZ = range(4)

        ctx1 = ExitStack()
        w_raw = sb("w_raw", [P, W_TOTAL], stack=ctx1)
        wk_raw = sb("wk_raw", [P, CK, C], stack=ctx1)
        wk_hi = sb("wk_hi", [P, CK, C], F32R, stack=ctx1)
        wk_lo = sb("wk_lo", [P, CK, C], F32R, stack=ctx1)
        wx_raw = sb("wx_raw", [P, CK, XA_W], stack=ctx1)
        wx_hi = sb("wx_hi", [P, CK, XA_W], F32R, stack=ctx1)
        wx_lo = sb("wx_lo", [P, CK, XA_W], F32R, stack=ctx1)
        attn_bc = sb("attn_bc", [P, 2, C], stack=ctx1)
        attn_prod = sb("attn_prod", [P, 2, CK, C], stack=ctx1)
        wv = sb("wv", [P, CK, C], stack=ctx1)
        wm = sb("wm", [P, CK, C], stack=ctx1)
        g1_col = sb("g1_col", [P, CK], stack=ctx1)
        b1_col = sb("b1_col", [P, CK], stack=ctx1)
        gw_raw = sb("gw_raw", [P, CK, EXPERTS], stack=ctx1)
        ob_raw = sb("ob_raw", [P, C], stack=ctx1)
        ob_hi = sb("ob_hi", [P, C], F32R, stack=ctx1)
        w2_nmean = sb("w2_nmean", [P, 4], stack=ctx1)
        head_mask = sb("head_mask", [P, P], stack=ctx1)
        xn1 = [sb(f"xn1_{n}", [R, T, C], stack=ctx1) for n in range(2)]
        xr_hi = [sb(f"xr_hi{n}", [R, T, KX_W], F32R, stack=ctx1) for n in range(2)]
        xr_lo = [sb(f"xr_lo{n}", [R, T, KX_W], F32R, stack=ctx1) for n in range(2)]
        x1T_hi = [sb(f"x1T_hi{n}", [P, CK, GR], F32R, stack=ctx1) for n in range(2)]
        x1T_lo = [sb(f"x1T_lo{n}", [P, CK, GR], F32R, stack=ctx1) for n in range(2)]
        kf = sb("kf", [R, T, C], stack=ctx1)
        k_hi = [sb(f"k_hi{n}", [R, T, C], F32R, stack=ctx1) for n in range(2)]
        k_lo = [sb(f"k_lo{n}", [R, T, C], F32R, stack=ctx1) for n in range(2)]
        xts = [sb(f"xts{n}", [R, T, XA_W], stack=ctx1) for n in range(2)]
        kx = sb("kx", [P, CK, KX_W], stack=ctx1)
        kxT = sb("kxT", [P, CK, C], stack=ctx1)
        kvT = sb("kvT", [P, CK, P], stack=ctx1)
        ctx1.close()

        row_n = sb("row_n", [R, T, C])
        row_z = sb("row_z", [R, T, C])
        base = sb("base", [R, T, C])
        xmid = [sb(f"xmid{n}", [R, T, C]) for n in range(2)]
        xT_hi = sb("xT_hi", [P, CK, GR], F32R)
        xT_lo = sb("xT_lo", [P, CK, GR], F32R)
        qf = sb("qf", [P, CK, GR])
        rden = sb("rden", [R, T, MIX_HEADS])
        rden_hi = sb("rden_hi", [R, T, MIX_HEADS], F32R)
        rdenT = sb("rdenT", [P, GR], F32R)
        mT_hi = sb("mT_hi", [P, CK, GR], F32R)
        mT_lo = sb("mT_lo", [P, CK, GR], F32R)
        h_hi = sb("h_hi", [P, 4, GR], F32R)
        h_lo = sb("h_lo", [P, 4, GR], F32R)
        z_hi = sb("z_hi", [P, CK, GR], F32R)
        z_lo = sb("z_lo", [P, CK, GR], F32R)
        s1_hi = sb("s1_hi", [P, 2, GR], F32R)
        s1_lo = sb("s1_lo", [P, 2, GR], F32R)
        e1_hi = sb("e1_hi", [P, 4, GR], F32R)
        e1_lo = sb("e1_lo", [P, 4, GR], F32R)
        s2_hi = sb("s2_hi", [P, GR], F32R)
        s2_lo = sb("s2_lo", [P, GR], F32R)
        relu = [sb(f"relu{n}", [P, 2, GR]) for n in range(3)]
        logits = sb("logits", [P, GR])
        idx = [sb(f"idx{n}", [R, 2, T], I32) for n in range(2)]
        xg = sb("xg", [R, T, XT_W])
        ag = sb("ag", [R, T, HEADS])
        soft = sb("soft", [R, 2, T, 4])
        soft_s = sb("soft_s", [R, 2, T])
        cmpb = sb("cmpb", [R, T, EXPERTS, 2, EXPERTS])
        rank = sb("rank", [R, T, EXPERTS])
        top_e = sb("top_e", [R, T, EXPERTS])
        top_s = sb("top_s", [R, T])
        top_hi = sb("top_hi", [R, T, EXPERTS], F32R)
        gateT = sb("gateT", [P, GR], F32R)
        gnn = sb("gnn", [R, T, HEAD_CH])

        psum = ctx.enter_context(nc.psum_tensor("psum", [P, 8, BANK], F32))

        def colT(b, n=None):
            return psum[:, b, 0:GR] if n is None else psum[:, b:b + n, 0:GR]

        def rowt(b, j, w=C):
            return psum[0:R, b + j // 2, (j % 2) * C:(j % 2) * C + w]

        def rows4(b):
            return psum[0:R, b:b + 2, :].rearrange("p b (j n) -> p (b j) n", j=2)

        def wslice(t, name, chunk, lo=0, n=None):
            at, cols = W_AT[name]
            at += chunk * cols + lo
            return t[:, at:at + (cols if n is None else n)]

        def split_mm(pe, out, w, x, first, last):
            (wh, wl), (xh, xl) = w, x
            pe.matmul(out, wh, xh, start=first, stop=False)
            pe.matmul(out, wh, xl, start=False, stop=False)
            return pe.matmul(out, wl, xh, start=False, stop=last)

        block = ctx.enter_context(nc.Block())

        def steps(eng, step, first, last):
            turns = (last - first) // 2
            with eng.Fori(first, first + 2 * turns, 2) as i:
                step(i, first % 2)
                step(i + 1, (first + 1) % 2)
            for i in range(first + 2 * turns, last):
                step(i, i % 2)

        def dma16(v, par):
            return 16 * (v // 2 + 1) if isinstance(v, int) else 8 * (v - par) + 16

        def load_idx(sp, v, par):
            sp.dma_start(idx[par][:, 0, :], src_rows[v]).then_inc(sem(f"idx{par}"), 16)
            sp.dma_start(idx[par][:, 1, :], dst_rows[v]).then_inc(sem(f"idx{par}"), 16)

        def wr(name, chunks):
            at, cols = W_AT[name]
            return w_raw[:, at:at + chunks * cols].rearrange("p (c n) -> p c n", c=chunks)

        def rows_of(name):
            return A[name].rearrange("(c p) n -> p c n", p=P)

        def column(name):
            return A[name].rearrange("(c p) -> p c", p=P)

        ew2 = W_AT["eW2"][0]
        ew2_raw = w_raw[:, ew2:ew2 + EXPERTS * P]
        ew2_halves = ew2_raw.rearrange("p (e m n) -> p e m n", e=EXPERTS, m=2)
        first_loads = [
            (wk_raw[:], rows_of("L0_mix_Wk")),
            (wx_raw[:, :, 0:C], rows_of("L0_gnn_weight")),
            (attn_bc[:, 0, :], A["L0_gnn_attn_r"].rearrange("h d -> (h d)").partition_broadcast(P)),
            (attn_bc[:, 1, :], A["L0_gnn_attn_l"].rearrange("h d -> (h d)").partition_broadcast(P)),
        ]
        later_loads = [
            (wr("Wq", 2), rows_of("L0_mix_Wq")), (wr("W1", 4), rows_of("L0_mix_W1")),
            (wr("W2", 4), rows_of("L0_mix_W2")), (wr("sW1", 2), rows_of("L0_ffn_sW1")),
            (wr("sW2", 2), rows_of("L0_ffn_sW2")), (wr("sW3", 1), rows_of("L0_ffn_sW3")),
            (wr("eW1", 8), A["L0_ffn_eW1"].rearrange("e (c p) n -> p (e c) n", p=P)),
            (wr("eW3", 2), A["L0_ffn_eW3"].rearrange("e g n -> (e g) n").rearrange("(q p) n -> p q n", p=P)),
            (wv[:], rows_of("L0_mix_Wv")), (wm[:], rows_of("L0_mix_Wm")), (gw_raw[:], rows_of("L0_ffn_gW")),
            (g1_col[:], column("L0_mix_g1")), (b1_col[:], column("L0_mix_b1")),
            (s1_bias[:], column("L0_ffn_sb1")), (s2_bias[:], column("L0_ffn_sb2")),
            (e1_bias[:], A["L0_ffn_eb1"].rearrange("e p -> p e")),
            (e2_bias[:], A["L0_ffn_eb2"].rearrange("e g -> (e g)").rearrange("(q p) -> p q", p=P)),
            (gate_bias[0:EXPERTS, :], A["L0_ffn_gb"].rearrange("(e o) -> e o", o=1)),
            (g2_bc[:], A["L0_mix_g2"].partition_broadcast(R)), (b2_bc[:], A["L0_mix_b2"].partition_broadcast(R)),
        ]
        later_loads += [(ew2_halves[:, e, e % 2, :], A["L0_ffn_eW2"][e]) for e in range(EXPERTS)]
        for at in (0, 32, 64):
            later_loads.append((ob_raw[at:at + EXPERTS, :], A["L0_ffn_eb3"]))
            later_loads.append((ob_raw[at + EXPERTS:at + EXPERTS + 1, :],
                                A["L0_ffn_sb3"].rearrange("(o n) -> o n", o=1)))

        plain_parts = [(0, W_AT["W1"][0] + 2 * 512), (W_AT["sW1"][0], W_AT["eW1"][0] + 2 * 128),
                       (W_AT["eW1"][0] + 2 * 128, W_TOTAL)]

        def enter_phase2(eng):
            for name in ("p1_pe", "p1_act", "p1_dve", "p1_pool", "tables"):
                need(eng, name, 1)

        @block.sync
        def _(sp):
            def load_x(v, par, prefix):
                sp.dma_start(xb[par][:], x_rows[v]).then_inc(sem(f"{prefix}{par}"), 16)

            load_x(0, 0, "x")
            for to, of in first_loads:
                sp.dma_start(to, of).then_inc(sem("w_first"), 16)
            load_x(1, 1, "x")
            need(sp, "zeroed", 1)
            for to, of in later_loads:
                sp.dma_start(to, of, allow_slow_non_contiguous=True).then_inc(sem("w_later"), 16)

            def phase1(v, par, more=True):
                if more:
                    need(sp, "xn1", v + 1)
                    load_x(v + 2, par, "x")
                need(sp, "xts", 2 * (v + 1))
                sp.dma_start(xt_rows[v], xts[par][:, :, 0:XT_W]).then_inc(sem(f"tab{par}"), 16)
                sp.dma_start(al_rows[v], xts[par][:, :, XT_W:XA_W]).then_inc(sem(f"tab{par}"), 16)
            steps(sp, phase1, 0, NG - 3)
            for v in range(NG - 3, NG):
                phase1(v, v % 2, more=v + 2 < NG)
            need(sp, "xn1", NG)
            load_x(0, 0, "y")
            load_x(1, 1, "y")
            need(sp, "tab0", 32 * ((NG + 1) // 2))
            need(sp, "tab1", 32 * (NG // 2))
            sp.nop().then_inc(sem("tables"), 1)
            enter_phase2(sp)
            load_idx(sp, 0, 0)
            load_idx(sp, 1, 1)

            def phase2(i, par, a=True, c=True, more=True):
                if a and more:
                    need(sp, "gath", 128 * (i + 1))
                    load_idx(sp, i + 2, par)
                if c:
                    need(sp, "out", i - 1)
                    sp.dma_start(out_rows[i - 2], xmid[par][:]).then_inc(sem(f"st{par}"), 16)
                if a and more:
                    need(sp, "t", i + 1)
                    load_x(i + 2, par, "y")
            phase2(0, 0, c=False)
            phase2(1, 1, c=False)
            steps(sp, phase2, 2, NG - 2)
            for i in range(NG - 2, NG + 2):
                phase2(i, i % 2, a=i < NG, more=False)
            need(sp, "st0", 16 * ((NG + 1) // 2))
            need(sp, "st1", 16 * (NG // 2))

        @block.tensor
        def _(pe):
            def transposes(src, b, done):
                for c in range(CK):
                    for j in range(T):
                        last = pe.transpose(psum[:, b + c, j * R:(j + 1) * R], src[:, j, c * P:(c + 1) * P],
                                            ident[0:R, 0:R])
                last.then_inc(sem(done), 1)

            def tile(t, c, j):
                return t[:, c, j * R:(j + 1) * R]

            def p1_transpose(v, par):
                need(pe, "xn1", v + 1)
                need(pe, "x1T", v)
                transposes(xn1[par], 0, "x1t")

            def p1_k(v, par):
                need(pe, "x1T", v + 1)
                need(pe, "kf", v)
                for j in range(T):
                    for c in range(CK):
                        last = split_mm(pe, rowt(2, j), (tile(x1T_hi[par], c, j), tile(x1T_lo[par], c, j)),
                                        (wk_hi[:, c, :], wk_lo[:, c, :]), c == 0, c == CK - 1)
                last.then_inc(sem("k_mm"), 1)

            def p1_table(v, par, pair):
                need(pe, "xts", 2 * v + pair)
                for j in (2 * pair, 2 * pair + 1):
                    for c in range(CK):
                        last = split_mm(pe, psum[0:R, 4 + j % 2, 0:XA_W],
                                        (tile(x1T_hi[par], c, j), tile(x1T_lo[par], c, j)),
                                        (wx_hi[:, c, :], wx_lo[:, c, :]), c == 0, c == CK - 1)
                last.then_inc(sem("xt_mm"), 1)

            def p1_kx(v, par, pair, first=False, last=False):
                if pair == 0:
                    need(pe, "k_split", v + 1)
                    need(pe, "x_split", v + 1)
                for j in (2 * pair, 2 * pair + 1):
                    for q in range(CK):
                        end = split_mm(pe, psum[:, 6 + q, 0:KX_W],
                                       (k_hi[par][:, j, q * P:(q + 1) * P], k_lo[par][:, j, q * P:(q + 1) * P]),
                                       (xr_hi[par][:, j, :], xr_lo[par][:, j, :]),
                                       first and j == 0, last and j == T - 1)
                if pair == 1:
                    end.then_inc(sem("kx"), 1)

            def phase1(v, par, kx=True, more=True):
                p1_k(v, par)
                if more:
                    p1_transpose(v + 1, 1 - par)
                for pair in range(2):
                    p1_table(v, par, pair)
                    if kx:
                        p1_kx(v - 1, 1 - par, pair, first=isinstance(v, int) and v == 1)

            need(pe, "ident", 1)
            p1_transpose(0, 0)
            need(pe, "w_split1", 1)
            phase1(0, 0, kx=False)
            phase1(1, 1)
            steps(pe, phase1, 2, NG - 1)
            phase1(NG - 1, (NG - 1) % 2, more=False)
            for pair in range(2):
                p1_kx(NG - 1, (NG - 1) % 2, pair, last=True)

            need(pe, "w_later", 16 * len(later_loads))
            for o in range(4):
                for c in range(CK):
                    last = pe.matmul(psum[:, 0, o:o + 1], wslice(w_raw, "W1", 2 + c, o * P, P), b1_col[:, c:c + 1],
                                     start=c == 0, stop=c == CK - 1)
            last.then_inc(sem("hb_mm"), 1)
            need(pe, "kxs", 1)
            for c in range(CK):
                for q in range(CK):
                    last = pe.transpose(psum[:, 2 + c, q * P:(q + 1) * P], kx[:, q, c * P:(c + 1) * P], ident[:])
            last.then_inc(sem("kxt_mm"), 1)
            need(pe, "kxT", 1)
            for q in range(CK):
                for c in range(CK):
                    last = pe.matmul(psum[:, 4, q * P:(q + 1) * P], wv[:, c, q * P:(q + 1) * P],
                                     kxT[:, c, q * P:(q + 1) * P], start=c == 0, stop=c == CK - 1)
            last.then_inc(sem("kv_mm"), 1)
            need(pe, "kvT", 1)
            for q in range(CK):
                last = pe.matmul(psum[:, 5, q * C:(q + 1) * C], kvT[:, q, :], wm[:, q, :], start=True, stop=True)
            last.then_inc(sem("p1_pe"), 1)

            def w1_part(half, o, b, x):
                for c in range(CK):
                    k = 2 * half + c
                    last = split_mm(pe, colT(b), (wslice(w_hi, "W1", k, o * P, P), wslice(w_lo, "W1", k, o * P, P)),
                                    (x[0][:, c, :], x[1][:, c, :]), k == 0, k == 3)
                return last

            def hidden(name, chunk, o, b, x, n=CK):
                for c in range(n):
                    last = split_mm(pe, colT(b), (wslice(w_hi, name, chunk + c, o * P, P),
                                                  wslice(w_lo, name, chunk + c, o * P, P)),
                                    (x[0][:, c, :], x[1][:, c, :]), c == 0, c == n - 1)
                return last

            def w2_pair(i, pair, c):
                if pair == 0:
                    need(pe, "h_lo", 2 * i)
                if c:
                    need(pe, *(("s1_relu", 2 * (i - 1)), ("e1_relu", 4 * (i - 2) + 1))[pair])
                for j in (2 * pair, 2 * pair + 1):
                    for k in range(4):
                        last = split_mm(pe, rowt(0, j), (tile(h_hi, k, j), tile(h_lo, k, j)),
                                        (wslice(w_hi, "W2", k), wslice(w_lo, "W2", k)), k == 0, k == 3)
                last.then_inc(sem("w2"), 1)

            def phase2(i, par, a=True, b=True, c=True):
                xT, mT, zT = (xT_hi, xT_lo), (mT_hi, mT_lo), (z_hi, z_lo)
                if b:
                    need(pe, "m_norm", i)
                    need(pe, "y", i - 1)
                    transposes(row_n, 0, "mt")
                    w1_part(0, 2, 6, xT)
                    w1_part(0, 3, 7, xT)
                    need(pe, "mT", i)
                    for o in range(2):
                        w1_part(1, o, 4 + o, mT).then_inc(sem("h_mm"), 1)
                if c:
                    need(pe, "z_norm", i - 1)
                    if not b:
                        need(pe, "y", i - 1)
                    transposes(row_z, 0, "zt")
                if b:
                    for o in range(2, 4):
                        w1_part(1, o, 4 + o, mT).then_inc(sem("h_mm"), 1)
                if a:
                    need(pe, "x_norm", i + 1)
                    need(pe, "out", i - 2)
                    transposes(row_n, 2, "xt2")
                if c:
                    need(pe, "zT", i - 1)
                    if b:
                        need(pe, "h_relu", 4 * (i - 1) + 1)
                    else:
                        need(pe, "e2g", i - 2)
                    for k, x in enumerate((z_hi, z_lo)):
                        for q in range(CK):
                            last = pe.matmul(colT(4), gate_w[:, q, :], x[:, q, :], start=k + q == 0, stop=k + q == 2)
                    last.then_inc(sem("lt"), 1)
                    if b:
                        need(pe, "h_relu", 4 * (i - 1) + 2)
                    hidden("sW1", 0, 0, 5, zT).then_inc(sem("s1_mm"), 1)
                    hidden("sW1", 0, 1, 0, zT).then_inc(sem("s1_mm"), 1)
                    need(pe, "lts", i - 1)
                    for j in range(T):
                        last = pe.transpose(psum[0:R, 4, j * P:(j + 1) * P], logits[:, j * R:(j + 1) * R], ident[:])
                    last.then_inc(sem("ltt"), 1)
                if a:
                    need(pe, "xT", i + 1)
                    if b:
                        need(pe, "h_relu", 4 * (i - 1) + 4)
                    for q in range(CK):
                        last = hidden("Wq", 0, q, 6 + q, xT)
                    last.then_inc(sem("q_mm"), 1)
                if c:
                    if not a:
                        need(pe, "out", i - 2)
                    for e in range(EXPERTS):
                        if e == 3:
                            need(pe, "l_read", i - 1)
                        hidden("eW1", 2 * e, 0, 1 + e, zT).then_inc(sem("e1_mm"), 1)
                if a:
                    need(pe, "q", i + 1)
                    for j in range(T):
                        for q in range(CK):
                            last = pe.matmul(psum[0:R, 6, j * MIX_HEADS:(j + 1) * MIX_HEADS], tile(qf, q, j),
                                             ksum_h[:, q, :], start=q == 0, stop=q == CK - 1)
                    last.then_inc(sem("den"), 1)
                for pair in range(2):
                    if b:
                        w2_pair(i, pair, c)
                    if a and pair == 0:
                        need(pe, "den_rows", i + 1)
                        for j in range(T):
                            last = pe.transpose(psum[:, 7, j * R:(j + 1) * R], den_rows[:, j, :], ident[0:R, 0:R])
                        last.then_inc(sem("dt"), 1)
                    if a and pair == 1:
                        need(pe, "rdenT", i + 1)
                        for q in range(CK):
                            last = pe.matmul(colT(6 + q), den_sel[:, q, :], rdenT[:], start=True, stop=True)
                        last.then_inc(sem("dx"), 1)
                if c:
                    need(pe, "gate_rows", i - 1)
                    need(pe, "s1_relu", 2 * (i - 1))
                    for j in range(T):
                        last = pe.transpose(psum[:, 5, j * R:(j + 1) * R], gate_rows[:, j, :], ident[0:R, 0:R])
                    last.then_inc(sem("gt"), 1)
                    need(pe, "s1_lo", i - 1)
                    need(pe, "e1_relu", 4 * (i - 1))
                    hidden("sW2", 0, 0, 4, (s1_hi, s1_lo)).then_inc(sem("s2_mm"), 1)
                    for q in range(2):
                        need(pe, "e1_lo", 2 * (i - 2) + q + 1)
                        for m in range(2):
                            e = 2 * q + m
                            last = split_mm(pe, colT(2 + q), (wslice(w_hi, "eW2", e), wslice(w_lo, "eW2", e)),
                                            (e1_hi[:, e, :], e1_lo[:, e, :]), m == 0, m == 1)
                        last.then_inc(sem("e2_mm"), 1)
                    need(pe, "gateT", i - 1)
                    need(pe, "s2_relu", i - 1)
                    for q in range(2):
                        last = pe.matmul(colT(4 + q), gate_sel[:, q, :], gateT[:], start=True, stop=True)
                    last.then_inc(sem("gb"), 1)
                if a:
                    need(pe, "qz", i + 1)
                    for j in range(T):
                        for q in range(CK):
                            last = split_mm(pe, rowt(6, j), (tile(z_hi, q, j), tile(z_lo, q, j)),
                                            (g_hi[:, q, :], g_lo[:, q, :]), q == 0, q == CK - 1)
                        if j % 2:
                            last.then_inc(sem("m_mm"), 1)
                    if c:
                        need(pe, "e2g", i - 1)
                    elif b:
                        need(pe, "h_relu", 4 * (i - 1) + 2)
                    w1_part(0, 0, 4, xT)
                    w1_part(0, 1, 5, xT)
                if c:
                    need(pe, "s2_lo", i - 1)
                    need(pe, "e2_relu", 2 * (i - 1))
                    for j in range(T):
                        out = rowt(2, j)
                        pe.matmul(out, gateT[:, j * R:(j + 1) * R], out_bias[:], start=True, stop=False)
                        split_mm(pe, out, (s2_hi[:, j * R:(j + 1) * R], s2_lo[:, j * R:(j + 1) * R]),
                                 (wslice(w_hi, "sW3", 0), wslice(w_lo, "sW3", 0)), False, False)
                        if j == 0:
                            need(pe, "e2_lo", i - 1)
                        for q in range(2):
                            last = split_mm(pe, out, (tile(h_hi, q, j), tile(h_lo, q, j)),
                                            (wslice(w_hi, "eW3", q), wslice(w_lo, "eW3", q)), False, q == 1)
                    last.then_inc(sem("out_mm"), 1)

            need(pe, "g_split", 1)
            phase2(0, 0, b=False, c=False)
            phase2(1, 1, c=False)
            phase2(2, 0)
            steps(pe, phase2, 3, NG)
            phase2(NG, NG % 2, a=False)
            phase2(NG + 1, (NG + 1) % 2, a=False, b=False)

        @block.scalar
        def _(act):
            def normalize(out, src, which, done):
                for j in range(T):
                    last = act.activation(out[:, j, :], src(j), ACT.Identity,
                                          bias=nm[which][:, j:j + 1], scale=rs[which][:, j:j + 1])
                last.then_inc(sem(done), 1)

            def p1_norm(v, par):
                need(act, "rs_x1", v + 1)
                need(act, "x1t", v - 1)
                need(act, "x_split", v - 1)
                normalize(xn1[par], lambda j: xb[par][:, j, :], LX, "xn1")

            def p1_copyT(v, par):
                need(act, "x1t", v + 1)
                need(act, "xt_mm", 2 * (v - 1))
                act.activation(x1T_hi[par][:], colT(0, 2), ACT.Copy).then_inc(sem("x1T_hi"), 1)

            def phase1(v, par, more=2):
                need(act, "k_mm", v + 1)
                need(act, "k_split", v)
                act.activation(kf[:], rows4(2), ACT.Exp).then_inc(sem("k_exp"), 1)
                if more >= 1:
                    p1_copyT(v + 1, 1 - par)
                for pair in range(2):
                    need(act, "xt_mm", 2 * v + pair + 1)
                    if pair == 0:
                        need(act, f"tab{par}", 2 * dma16(v - 2, par))
                    act.activation(xts[par][:, 2 * pair:2 * pair + 2, :], psum[0:R, 4:6, 0:XA_W],
                                   ACT.Copy).then_inc(sem("xts"), 1)
                if more >= 2:
                    p1_norm(v + 2, par)

            p1_norm(0, 0)
            p1_norm(1, 1)
            p1_copyT(0, 0)
            phase1(0, 0)
            phase1(1, 1)
            steps(act, phase1, 2, NG - 3)
            need(act, "w_later", 16 * len(later_loads))
            for v in range(NG - 3, NG):
                phase1(v, v % 2, more=NG - 1 - v)
                if v == NG - 2:
                    need(act, "w2_mean", 1)
                    for k in range(4):
                        act.activation(wslice(w_hi, "W2", k), wslice(w_raw, "W2", k), ACT.Identity,
                                       bias=w2_nmean[:, k:k + 1])
                if v == NG - 1:
                    for c in range(CK):
                        act.activation(wslice(w_hi, "W1", 2 + c), wslice(w_raw, "W1", 2 + c), ACT.Identity,
                                       scale=g1_col[:, c:c + 1])
                lo, hi = plain_parts[v - (NG - 3)]
                act.activation(w_hi[:, lo:hi], w_raw[:, lo:hi], ACT.Copy).then_inc(sem("w_hi"), 1)

            need(act, "kxt_mm", 1)
            act.activation(kxT[:], psum[:, 2:4, 0:C], ACT.Copy).then_inc(sem("kxT"), 1)
            need(act, "p1_pe", 1)
            act.activation(g_hi[:], psum[:, 5, :].rearrange("p (q n) -> p q n", q=CK), ACT.Copy).then_inc(sem("g_hi"), 1)
            act.nop().then_inc(sem("p1_act"), 1)

            def relu_split(out, hi, b, bias, count, mm, done):
                need(act, mm, count)
                act.activation(out, colT(b), ACT.Relu, bias=bias)
                act.activation(hi, colT(b), ACT.Relu, bias=bias).then_inc(sem(done), 1)

            def soft_part(a, c):
                return soft[:, 0 if c else 1:2 if a else 1, :, :]

            def phase2(i, par, a=True, b=True, c=True):
                if b:
                    need(act, "mt", i)
                    act.activation(mT_hi[:], colT(0, 2), ACT.Copy).then_inc(sem("mT_hi"), 1)
                if a:
                    need(act, "rs_x", i + 1)
                    if b:
                        need(act, "mt", i)
                    normalize(row_n, lambda j: xb[par][:, j, :], LX, "x_norm")
                if b:
                    need(act, "e2_lo", i - 2)
                    for o in range(2):
                        relu_split(relu[0][:, o, :], h_hi[:, o, :], 4 + o, h_bias[:, o:o + 1],
                                   4 * (i - 1) + o + 1, "h_mm", "h_relu")
                if c:
                    need(act, "zt", i - 1)
                    act.activation(z_hi[:], colT(0, 2), ACT.Copy).then_inc(sem("z_hi"), 1)
                if b:
                    need(act, "e1_lo", 2 * (i - 2))
                    for o in range(2, 4):
                        relu_split(relu[1][:, o - 2, :], h_hi[:, o, :], 4 + o, h_bias[:, o:o + 1],
                                   4 * (i - 1) + o + 1, "h_mm", "h_relu")
                if a:
                    need(act, "xt2", i + 1)
                    act.activation(xT_hi[:], colT(2, 2), ACT.Copy).then_inc(sem("xT_hi"), 1)
                if c:
                    need(act, "lt", i - 1)
                    act.activation(logits[:], colT(4), ACT.Identity, bias=gate_bias[:, 0:1]).then_inc(sem("lts"), 1)
                    need(act, "s2_lo", i - 2)
                    for o in range(2):
                        relu_split(relu[2][:, o, :], s1_hi[:, o, :], 5 if o == 0 else 0, s1_bias[:, o:o + 1],
                                   2 * (i - 2) + o + 1, "s1_mm", "s1_relu")
                if a or c:
                    need(act, "soft_sub", i + 1)
                    act.activation(soft_part(a, c), soft_part(a, c), ACT.Exp).then_inc(sem("soft_exp"), 1)
                if a:
                    need(act, "q_mm", i + 1)
                    need(act, "qz", i)
                    act.activation(qf[:], colT(6, 2), ACT.Exp).then_inc(sem("q_exp"), 1)
                if c:
                    for e in range(EXPERTS):
                        if e == 0:
                            need(act, *(("h_lo", 2 * (i - 1) + 1) if b else ("e2_lo", i - 2)))
                        if e == 2:
                            need(act, *(("h_lo", 2 * (i - 1) + 2) if b else ("e1_lo", 2 * (i - 2))))
                        relu_split(relu[e // 2][:, e % 2, :], e1_hi[:, e, :], 1 + e, e1_bias[:, e:e + 1],
                                   4 * (i - 2) + e + 1, "e1_mm", "e1_relu")
                        if e == 1:
                            need(act, "gates", i - 1)
                            act.activation(top_e[:], soft[:, 0, :, :], ACT.Exp).then_inc(sem("top_exp"), 1)
                if a:
                    need(act, "dt", i + 1)
                    act.activation(rdenT[:], colT(7), ACT.Copy).then_inc(sem("rdenT"), 1)
                if c:
                    need(act, "gt", i - 1)
                    act.activation(gateT[:], colT(5), ACT.Copy).then_inc(sem("gateT"), 1)
                if a:
                    need(act, "q_den", i + 1)
                    act.activation(z_hi[:], qf[:], ACT.Copy).then_inc(sem("qz_hi"), 1)
                if c:
                    need(act, "s1_lo", i - 1)
                    relu_split(relu[2][:, 0, :], s2_hi[:], 4, s2_bias[:, 0:1], i - 1, "s2_mm", "s2_relu")
                    need(act, "e1_lo", 2 * (i - 2) + 1)
                    for q in range(2):
                        need(act, "e2_mm", 2 * (i - 2) + q + 1)
                        act.activation(relu[0][:, q, :], colT(2 + q), ACT.Relu,
                                       bias=e2_bias[:, q:q + 1]).then_inc(sem("e2_relu"), 1)
                    need(act, "e2g", i - 1)
                    act.activation(h_hi[:, 0:2, :], relu[0][:], ACT.Copy).then_inc(sem("e2_hi"), 1)
                if a:
                    need(act, "rs_m", i + 1)
                    need(act, "xt2", i + 1)
                    normalize(row_n, lambda j: rowt(6, j), LM, "m_norm")
                if b:
                    need(act, "rs_z", i)
                    need(act, "zt", i - 1)
                    normalize(row_z, lambda j: xmid[1 - par][:, j, :], LZ, "z_norm")

            enter_phase2(act)
            phase2(0, 0, b=False, c=False)
            phase2(1, 1, c=False)
            phase2(2, 0)
            steps(act, phase2, 3, NG)
            phase2(NG, NG % 2, a=False)
            phase2(NG + 1, (NG + 1) % 2, a=False, b=False)

        @block.vector
        def _(dve):
            tt, ts, stt = dve.tensor_tensor, dve.tensor_scalar, dve.scalar_tensor_tensor

            def stats(tiles, src):
                for j in tiles:
                    dve.bn_stats(bn[:, j, :], src(j))

            def aggregate(which, done):
                dve.drain()
                for j in range(T):
                    last = dve.bn_aggr(mv[which][:, j, :], bn[:, j, :])
                last.then_inc(sem(done), 1)

            def p1_stats(v, par):
                dve.drain()
                need(dve, f"x{par}", dma16(v, par))
                need(dve, "rs_x1", v)
                stats(range(T), lambda j: xb[par][:, j, :])
                aggregate(LX, "mv_x1")

            p1_stats(0, 0)
            need(dve, "w_first", 16 * len(first_loads))
            dve.tensor_copy(wk_hi[:], wk_raw[:])
            for s in range(2):
                tt(attn_prod[:, s, :, :], wx_raw[:, :, 0:C],
                   attn_bc[:, s, :].unsqueeze(1).broadcast_to([P, CK, C]), ALU.mult)
            dve.drain()
            tt(wk_lo[:], wk_raw[:], wk_hi[:], ALU.subtract)
            for s in range(2):
                dve.reduce_sum(wx_raw[:, :, C + HEADS * s:C + HEADS * (s + 1)],
                               attn_prod[:, s, :, :].rearrange("p c (h d) -> p c h d", h=HEADS), AXX)
            dve.drain()
            dve.tensor_copy(wx_hi[:], wx_raw[:])
            dve.drain()
            tt(wx_lo[:], wx_raw[:], wx_hi[:], ALU.subtract).then_inc(sem("w_split1"), 1)
            p1_stats(1, 1)

            def p1_lowT(v, par):
                need(dve, "x1T_hi", v + 1)
                tt(x1T_lo[par][:], colT(0, 2), x1T_hi[par][:], ALU.subtract).then_inc(sem("x1T"), 1)

            def phase1(v, par, more=2):
                if more >= 2:
                    p1_stats(v + 2, par)
                need(dve, "kx", v - 1)
                need(dve, "xn1", v + 1)
                if isinstance(v, int) and v < 2:
                    need(dve, "xr_ones", 1)
                dve.tensor_copy(xr_hi[par][:, :, 0:C], xn1[par][:]).then_inc(sem("xr_hi"), 1)
                need(dve, "k_exp", v + 1)
                ts(kf[:], kf[:], 1.0, None, ALU.min)
                if more >= 1:
                    p1_lowT(v + 1, 1 - par)
                dve.drain()
                stt(kf[:], rows4(2), 1.0, kf[:], ALU.add, ALU.max).then_inc(sem("kf"), 1)
                dve.drain()
                dve.tensor_copy(k_hi[par][:], kf[:]).then_inc(sem("k_hi"), 1)

            p1_lowT(0, 0)
            phase1(0, 0)
            phase1(1, 1)
            steps(dve, phase1, 2, NG - 3)

            w2 = w_raw[:, W_AT["W2"][0]:W_AT["W2"][0] + 4 * C].rearrange("p (k n) -> p k n", k=4)

            def small_constants():
                dve.memset(head_mask[:], 0.0)
                dve.memset(ksum_h[:], 0.0)
                dve.drain()
                for h in range(P // MIX_CH):
                    dve.memset(head_mask[h * MIX_CH:(h + 1) * MIX_CH, h * MIX_CH:(h + 1) * MIX_CH], 1.0)
                need(dve, "w_later", 16 * len(later_loads))
                for e in range(EXPERTS):
                    tt(gate_sel[:, e // 2, e % 2 * HEAD_CH:(e % 2 + 1) * HEAD_CH],
                       ident[:, e:e + 1].broadcast_to([P, HEAD_CH]),
                       ident[:, 32 + e:33 + e].broadcast_to([P, HEAD_CH]), ALU.add)
                per = MIX_HEADS // CK
                for h in range(MIX_HEADS):
                    tt(den_sel[:, h // per, h % per * MIX_CH:(h % per + 1) * MIX_CH],
                       ident[:, h:h + 1].broadcast_to([P, MIX_CH]),
                       ident[:, 32 + h:33 + h].broadcast_to([P, MIX_CH]), ALU.add)
                need(dve, "zeroed", 1)
                dve.tensor_copy(gate_w[:, :, 0:EXPERTS], gw_raw[:])
                for at in (0, 32):
                    dve.tensor_copy(out_bias[at:at + EXPERTS + 1, :], ob_raw[at:at + EXPERTS + 1, :])
                dve.tensor_copy(ob_hi[64:64 + EXPERTS + 1, :], ob_raw[64:64 + EXPERTS + 1, :])
                dve.reduce_sum(w2_nmean[:], w2, AXX)
                dve.drain()
                ts(w2_nmean[:], w2_nmean[:], -1.0 / C, None, ALU.mult).then_inc(sem("w2_mean"), 1)
                tt(gate_w[:, :, EXPERTS:2 * EXPERTS], gw_raw[:], gate_w[:, :, 0:EXPERTS], ALU.subtract)
                tt(out_bias[64:64 + EXPERTS + 1, :], ob_raw[64:64 + EXPERTS + 1, :], ob_hi[64:64 + EXPERTS + 1, :],
                   ALU.subtract)

            def second_parts(n):
                need(dve, "w_hi", n + 1)
                lo, hi = plain_parts[n]
                tt(w_lo[:, lo:hi], w_raw[:, lo:hi], w_hi[:, lo:hi], ALU.subtract)
                if n == 1:
                    for k in range(4):
                        stt(wslice(w_lo, "W2", k), wslice(w_raw, "W2", k), w2_nmean[:, k:k + 1],
                            wslice(w_hi, "W2", k), ALU.add, ALU.subtract)
                if n == 2:
                    for c in range(CK):
                        stt(wslice(w_lo, "W1", 2 + c), wslice(w_raw, "W1", 2 + c), g1_col[:, c:c + 1],
                            wslice(w_hi, "W1", 2 + c), ALU.mult, ALU.subtract)

            for v in range(NG - 3, NG):
                phase1(v, v % 2, more=NG - 1 - v)
                if v == NG - 3:
                    small_constants()
                else:
                    second_parts(v - (NG - 3) - 1)

            need(dve, "kx", NG)
            dve.tensor_copy(kx[:], psum[:, 6:8, 0:KX_W]).then_inc(sem("kxs"), 1)
            need(dve, "hb_mm", 1)
            dve.tensor_copy(h_bias[:], psum[:, 0, 0:4])
            dve.drain()
            per = MIX_HEADS // CK
            for q in range(CK):
                ts(ksum_h[:, q, q * per:(q + 1) * per], head_mask[:, 0:P:MIX_CH], kx[:, q, C:C + 1], None, ALU.mult)
            need(dve, "kv_mm", 1)
            for q in range(CK):
                last = tt(kvT[:, q, :], psum[:, 4, q * P:(q + 1) * P], head_mask[:], ALU.mult)
            last.then_inc(sem("kvT"), 1)
            second_parts(2)
            need(dve, "g_hi", 1)
            tt(g_lo[:], psum[:, 5, :].rearrange("p (q n) -> p q n", q=CK), g_hi[:],
               ALU.subtract).then_inc(sem("g_split"), 1)
            dve.nop().then_inc(sem("p1_dve"), 1)

            def soft_chain_in(i, a, c):
                lt = psum[0:R, 4, :].rearrange("p (j n) -> p j n", j=T)
                if c:
                    need(dve, "ltt", i - 1)
                    dve.tensor_copy(soft[:, 0, :, :], lt[:, :, EXPERTS:2 * EXPERTS])
                if a:
                    need(dve, "gath", 128 * (i + 1))
                    tt(soft[:, 1, :, :], ag[:], xg[:, :, C:C + HEADS], ALU.add)
                dve.drain()
                if c:
                    tt(soft[:, 0, :, :], lt[:, :, 0:EXPERTS], soft[:, 0, :, :], ALU.add).then_inc(sem("l_read"), 1)
                if a:
                    stt(soft[:, 1, :, :], soft[:, 1, :, :], 0.01, soft[:, 1, :, :], ALU.mult, ALU.max)
                s, m = soft_views(a, c)
                dve.drain()
                dve.reduce_max(m, s, AXX)
                dve.drain()
                tt(s, s, m.unsqueeze(3).broadcast_to(s.shape), ALU.subtract).then_inc(sem("soft_sub"), 1)

            def soft_views(a, c):
                lo, hi = (0 if c else 1), (2 if a else 1)
                return soft[:, lo:hi, :, :], soft_s[:, lo:hi, :]

            def soft_chain_out(i, a, c):
                s, m = soft_views(a, c)
                need(dve, "soft_exp", i + 1)
                dve.reduce_sum(m, s, AXX)
                dve.drain()
                dve.reciprocal(m, m)
                dve.drain()
                last = tt(s, s, m.unsqueeze(3).broadcast_to(s.shape), ALU.mult)
                if c:
                    last.then_inc(sem("gates"), 1)
                dve.drain()

            def compare(i):
                g = soft[:, 0, :, :]
                for n, op in enumerate((ALU.is_ge, ALU.is_gt)):
                    tt(cmpb[:, :, :, n, :], g.unsqueeze(2).broadcast_to([R, T, EXPERTS, EXPERTS]),
                       g.unsqueeze(3).broadcast_to([R, T, EXPERTS, EXPERTS]), op)
                dve.drain()
                cm = cmpb[:].rearrange("p t e n j -> p t (e n j)")
                tt(cm, cm, beats[:].rearrange("p e n j -> p (e n j)").unsqueeze(1).broadcast_to(
                    [R, T, 2 * EXPERTS * EXPERTS]), ALU.mult)
                dve.drain()
                dve.reduce_sum(rank[:], cmpb[:].rearrange("p t e n j -> p t e (n j)"), AXX)

            def top_weights(i):
                dve.drain()
                need(dve, "top_exp", i - 1)
                need(dve, "gt", i - 2)
                stt(top_e[:], rank[:], float(TOPK), top_e[:], ALU.is_lt, ALU.mult)
                dve.drain()
                dve.reduce_sum(top_s[:], top_e[:], AXX)
                dve.drain()
                dve.reciprocal(top_s[:], top_s[:])
                dve.drain()
                tt(top_e[:], top_e[:], top_s[:].unsqueeze(2).broadcast_to([R, T, EXPERTS]), ALU.mult)
                dve.drain()
                dve.tensor_copy(top_hi[:], top_e[:])
                dve.drain()
                for at in (0, 64):
                    dve.tensor_copy(gate_rows[:, :, at:at + EXPERTS], top_hi[:])
                tt(gate_rows[:, :, 32:32 + EXPERTS], top_e[:], top_hi[:], ALU.subtract).then_inc(sem("gate_rows"), 1)

            def one_over_den(i):
                need(dve, "den", i + 1)
                ts(rden[:], psum[0:R, 6, 0:T * MIX_HEADS].rearrange("p (j h) -> p j h", j=T), ATT_EPS, None, ALU.add)
                dve.drain()
                dve.reciprocal(rden[:], rden[:])
                dve.drain()
                dve.tensor_copy(rden_hi[:], rden[:])
                dve.drain()
                dve.tensor_copy(den_rows[:, :, 0:MIX_HEADS], rden_hi[:])
                tt(den_rows[:, :, 32:32 + MIX_HEADS], rden[:], rden_hi[:], ALU.subtract).then_inc(sem("den_rows"), 1)

            def graph_layer(i):
                need(dve, "base", i)
                for h in range(HEADS):
                    for j in range(T):
                        part = xg[:, j, h * HEAD_CH:(h + 1) * HEAD_CH]
                        al = soft[:, 1, j, h:h + 1]
                        if h == 0:
                            last = ts(gnn[:, j, :], part, al, nm[LX][:, j:j + 1], ALU.mult, ALU.add)
                        else:
                            last = stt(gnn[:, j, :], part, al, gnn[:, j, :], ALU.mult, ALU.add)
                    if h == HEADS - 1:
                        last.then_inc(sem("gnn"), 1)
                    dve.drain()

            def phase2(i, par, a=True, b=True, c=True):
                if a:
                    dve.drain()
                    need(dve, f"y{par}", dma16(i, par))
                    need(dve, "rs_x", i)
                    stats(range(T), lambda j: xb[par][:, j, :])
                    aggregate(LX, "mv_x")
                if b:
                    need(dve, "mT_hi", i)
                    tt(mT_lo[:], colT(0, 2), mT_hi[:], ALU.subtract).then_inc(sem("mT"), 1)
                if c:
                    need(dve, "z_hi", i - 1)
                    tt(z_lo[:], colT(0, 2), z_hi[:], ALU.subtract).then_inc(sem("zT"), 1)
                if a:
                    need(dve, "xT_hi", i + 1)
                    tt(xT_lo[:], colT(2, 2), xT_hi[:], ALU.subtract).then_inc(sem("xT"), 1)
                if a or c:
                    soft_chain_in(i, a, c)
                    soft_chain_out(i, a, c)
                if c:
                    compare(i)
                if a:
                    need(dve, "q_exp", i + 1)
                    ts(qf[:], qf[:], 1.0, None, ALU.min)
                    dve.drain()
                    stt(qf[:], colT(6, 2), 1.0, qf[:], ALU.add, ALU.max).then_inc(sem("q"), 1)
                if c:
                    top_weights(i)
                if a:
                    one_over_den(i)
                    graph_layer(i)
                if b:
                    need(dve, "w2", 2 * i - 1)
                    need(dve, "rs_y", i - 1)
                    stats((0, 1), lambda j: rowt(0, j))
                if a:
                    need(dve, "dx", i + 1)
                    tt(qf[:], qf[:], colT(6, 2), ALU.mult).then_inc(sem("q_den"), 1)
                if b:
                    need(dve, "w2", 2 * i)
                    stats((2, 3), lambda j: rowt(0, j))
                    aggregate(LY, "mv_y")
                if a:
                    need(dve, "qz_hi", i + 1)
                    tt(z_lo[:], qf[:], z_hi[:], ALU.subtract).then_inc(sem("qz"), 1)
                if b:
                    need(dve, "rs_y", i)
                    need(dve, f"st{1 - par}", dma16(i - 3, 1 - par))
                    for j in range(T):
                        last = stt(xmid[1 - par][:, j, :], rowt(0, j), rs[LY][:, j:j + 1], g2_bc[:],
                                   ALU.mult, ALU.mult)
                    last.then_inc(sem("y"), 1)
                if c:
                    need(dve, "e2_relu", 2 * (i - 1))
                    need(dve, "gb", i - 1)
                    tt(relu[0][:], relu[0][:], colT(4, 2), ALU.mult).then_inc(sem("e2g"), 1)
                if a:
                    dve.drain()
                    need(dve, "rs_m", i)
                    for pair in range(2):
                        need(dve, "m_mm", 2 * i + pair + 1)
                        stats((2 * pair, 2 * pair + 1), lambda j: rowt(6, j))
                    aggregate(LM, "mv_m")
                if c:
                    need(dve, "e2_hi", i - 1)
                    tt(h_lo[:, 0:2, :], relu[0][:], h_hi[:, 0:2, :], ALU.subtract).then_inc(sem("e2_lo"), 1)
                if b:
                    dve.drain()
                    need(dve, "base", i)
                    tt(xmid[1 - par][:], xmid[1 - par][:], base[:], ALU.add).then_inc(sem("xmid"), 1)
                    dve.drain()
                    need(dve, "rs_z", i - 1)
                    stats(range(T), lambda j: xmid[1 - par][:, j, :])
                    aggregate(LZ, "mv_z")
                if a:
                    dve.drain()
                    for j in range(T):
                        last = stt(base[:, j, :], xb[par][:, j, :], rs1[:, j:j + 1], b2_bc[:], ALU.mult, ALU.add)
                    last.then_inc(sem("t"), 1)
                if c:
                    need(dve, "out_mm", i - 1)
                    tt(xmid[par][:], xmid[par][:], rows4(2), ALU.add).then_inc(sem("out"), 1)

            enter_phase2(dve)
            need(dve, "masks", 1)
            phase2(0, 0, b=False, c=False)
            phase2(1, 1, c=False)
            phase2(2, 0)
            steps(dve, phase2, 3, NG)
            phase2(NG, NG % 2, a=False)
            phase2(NG + 1, (NG + 1) % 2, a=False, b=False)

        @block.gpsimd
        def _(pool):
            ptt, pts = pool.tensor_tensor, pool.tensor_scalar

            def rstd(which, mvs, count, done, plus_one=False):
                need(pool, mvs, count)
                ptt(veps[which][:], mv[which][:, :, 1], eps[:], ALU.add)
                pts(nmean[which][:], mv[which][:, :, 0], -1.0, None, ALU.mult)
                pool.drain()
                ptt(rs[which][:], veps[which][:], neg_half[:], ALU.pow)
                pool.drain()
                if plus_one:
                    pts(rs1[:], rs[which][:], 1.0, None, ALU.add)
                ptt(nm[which][:], nmean[which][:], rs[which][:], ALU.mult).then_inc(sem(done), 1)

            pool.memset(ident[:], 0.0)
            pool.memset(neg_half[:], -0.5)
            pool.memset(eps[:], LN_EPS)
            pool.drain()
            pool.affine_select(out=ident[:], in_=ident[:], compare_op=ALU.not_equal, fill=1.0, base=0,
                               pattern=[[-1, P]], channel_multiplier=1).then_inc(sem("ident"), 1)
            rstd(LX, "mv_x1", 1, "rs_x1")
            pool.memset(ew2_raw, 0.0)
            pool.memset(gate_bias[:], 0.0)
            pool.memset(gate_w[:].bitcast(F32), 0.0)
            pool.memset(out_bias[:].bitcast(F32), 0.0).then_inc(sem("zeroed"), 1)
            for n in range(2):
                pool.memset(xr_hi[n][:, :, C:C + 1].bitcast(F32), 1.0)
                pool.memset(xr_hi[n][:, :, C + 1:C + 2].bitcast(F32), 0.0)
                last = pool.memset(xr_lo[n][:, :, C:C + 2].bitcast(F32), 0.0)
            last.then_inc(sem("xr_ones"), 1)

            def p1_rstd(v):
                need(pool, "xn1", v)
                rstd(LX, "mv_x1", v + 1, "rs_x1")

            def phase1(v, par, more=True):
                if more:
                    p1_rstd(v + 2)
                need(pool, "xr_hi", v + 1)
                need(pool, "kx", v - 1)
                ptt(xr_lo[par][:, :, 0:C], xn1[par][:], xr_hi[par][:, :, 0:C], ALU.subtract).then_inc(sem("x_split"), 1)
                need(pool, "k_hi", v + 1)
                ptt(k_lo[par][:], kf[:], k_hi[par][:], ALU.subtract).then_inc(sem("k_split"), 1)

            p1_rstd(1)
            phase1(0, 0)
            pool.memset(beats[:], 1.0)
            pool.memset(gate_rows[:], 0.0)
            pool.memset(den_rows[:], 0.0)
            pool.drain()
            for at in (0, 64):
                pool.memset(gate_rows[:, :, at + EXPERTS:at + EXPERTS + 1], 1.0)
            for n, sign in ((0, 1), (1, -1)):
                last = pool.affine_select(out=beats[:, :, n, :], in_=beats[:, :, n, :], compare_op=ALU.is_gt, fill=0.0,
                                          base=0, pattern=[[sign, EXPERTS], [-sign, EXPERTS]], channel_multiplier=0)
            last.then_inc(sem("masks"), 1)
            phase1(1, 1)
            steps(pool, phase1, 2, NG - 3)
            for v in range(NG - 3, NG):
                phase1(v, v % 2, more=v + 2 < NG)
            pool.nop().then_inc(sem("p1_pool"), 1)

            def low(out, src, hi, done):
                ptt(out, src, hi, ALU.subtract).then_inc(sem(done), 1)

            def phase2(i, par, a=True, b=True, c=True):
                if a:
                    need(pool, f"idx{par}", 2 * dma16(i, par))
                    need(pool, "t", i)
                    need(pool, "gnn", i)
                    rstd(LX, "mv_x", i + 1, "rs_x", plus_one=True)
                    for j in range(T):
                        pool.indirect_dma_start(xg[:, j, :], None, table_xt.ap(), bass.IndirectOffsetOnAxis(
                            idx[par][:, 1, j:j + 1], 0)).then_inc(sem("gath"), 16)
                        pool.indirect_dma_start(ag[:, j, :], None, table_al.ap(), bass.IndirectOffsetOnAxis(
                            idx[par][:, 0, j:j + 1], 0)).then_inc(sem("gath"), 16)
                if b:
                    for n in range(2):
                        need(pool, "h_relu", 4 * (i - 1) + 2 * n + 2)
                        low(h_lo[:, 2 * n:2 * n + 2, :], relu[n][:], h_hi[:, 2 * n:2 * n + 2, :], "h_lo")
                if c:
                    need(pool, "s1_relu", 2 * (i - 1))
                    low(s1_lo[:], relu[2][:], s1_hi[:], "s1_lo")
                if b:
                    need(pool, "t", i)
                    need(pool, "gnn", i)
                    bv = base[:].rearrange("p j (h d) -> p j h d", h=HEADS)
                    ptt(bv, bv, gnn[:].unsqueeze(2).broadcast_to([R, T, HEADS, HEAD_CH]),
                        ALU.add).then_inc(sem("base"), 1)
                if c:
                    for n in range(2):
                        need(pool, "e1_relu", 4 * (i - 2) + 2 * n + 2)
                        low(e1_lo[:, 2 * n:2 * n + 2, :], relu[n][:], e1_hi[:, 2 * n:2 * n + 2, :], "e1_lo")
                if b:
                    need(pool, "y", i - 1)
                    rstd(LY, "mv_y", i, "rs_y")
                if c:
                    need(pool, "s2_relu", i - 1)
                    low(s2_lo[:], relu[2][:, 0, :], s2_hi[:], "s2_lo")
                if a:
                    need(pool, "m_norm", i)
                    rstd(LM, "mv_m", i + 1, "rs_m")
                if b:
                    need(pool, "z_norm", i - 1)
                    rstd(LZ, "mv_z", i, "rs_z")

            enter_phase2(pool)
            phase2(0, 0, b=False, c=False)
            phase2(1, 1, c=False)
            phase2(2, 0)
            steps(pool, phase2, 3, NG)
            phase2(NG, NG % 2, a=False)
            phase2(NG + 1, (NG + 1) % 2, a=False, b=False)


_INS = ["x", "src", "dst", "L0_gnn_weight", "L0_gnn_attn_l", "L0_gnn_attn_r", "L0_mix_Wq", "L0_mix_Wk", "L0_mix_Wv",
        "L0_mix_Wm", "L0_mix_W1", "L0_mix_W2", "L0_mix_g1", "L0_mix_b1", "L0_mix_g2", "L0_mix_b2", "L0_ffn_sW1",
        "L0_ffn_sb1", "L0_ffn_sW2", "L0_ffn_sb2", "L0_ffn_sW3", "L0_ffn_sb3", "L0_ffn_eW1", "L0_ffn_eb1",
        "L0_ffn_eW2", "L0_ffn_eb2", "L0_ffn_eW3", "L0_ffn_eb3", "L0_ffn_gW", "L0_ffn_gb"]


def kernel(**inputs):
    import numpy as np
    import concourse.bacc as bacc
    from concourse.bass_utils import run_bass_kernel_spmd

    nc = bacc.Bacc("TRN2", target_bir_lowering=False, num_devices=1)
    arrays, aps = {}, {}
    for name in _INS:
        a = np.ascontiguousarray(inputs[name])
        arrays[f"in_{name}"] = a
        aps[name] = nc.dram_tensor(f"in_{name}", a.shape, mybir.dt.from_np(a.dtype), kind="ExternalInput").ap()
    aps["out"] = nc.dram_tensor("out_0", (N_NODES, C), F32, kind="ExternalOutput").ap()
    gps_layer(nc, aps)
    r = run_bass_kernel_spmd(nc, [arrays], core_ids=[0])
    return r.results[0]["out_0"]
```

```python
from contextlib import ExitStack

import concourse.bass as bass
from concourse import mybir

F32 = mybir.dt.float32
F32R = mybir.dt.float32r
I32 = mybir.dt.int32
ALU = mybir.AluOpType
ACT = mybir.ActivationFunctionType
AXX = mybir.AxisListType.X

N_NODES = 12500
C = 256
HEADS, HEAD_CH = 4, 64
MIX_HEADS, MIX_CH = 8, 32
EXPERTS, TOPK = 4, 2
LN_EPS, ATT_EPS = 1e-5, 1e-6

P = 128
R = 125
T = 4
GR = R * T
NG = N_NODES // GR
CK = C // P
BANK = 512
XT_W = C + HEADS
XA_W = XT_W + HEADS
KX_W = C + 2

W_AT, W_TOTAL = {}, 0
for _name, _chunks, _cols in (("Wq", 2, 256), ("W1", 4, 512), ("W2", 4, 256), ("sW1", 2, 256), ("sW2", 2, 128),
                              ("sW3", 1, 256), ("eW1", 8, 128), ("eW2", 4, 128), ("eW3", 2, 256)):
    W_AT[_name] = (W_TOTAL, _cols)
    W_TOTAL += _chunks * _cols


def gps_layer(nc, A):
    ctx = ExitStack()
    with ctx:
        def sb(name, shape, dt=F32, stack=ctx):
            return stack.enter_context(nc.sbuf_tensor(name, shape, dt))

        sems = {}

        def sem(name):
            if name not in sems:
                sems[name] = ctx.enter_context(nc.semaphore("s_" + name))
            return sems[name]

        def need(eng, name, count):
            if not (isinstance(count, int) and count <= 0):
                eng.wait_ge(sem(name), count)

        table_xt = nc.dram_tensor("table_xt", [N_NODES, XT_W], F32)
        table_al = nc.dram_tensor("table_al", [N_NODES, HEADS], F32)
        xt_rows = table_xt.ap().rearrange("(g p j) n -> g p j n", p=R, j=T)
        al_rows = table_al.ap().rearrange("(g p j) n -> g p j n", p=R, j=T)
        x_rows = A["x"].rearrange("(g p j) n -> g p j n", p=R, j=T)
        out_rows = A["out"].rearrange("(g p j) n -> g p j n", p=R, j=T)
        src_rows = A["src"][0:N_NODES].rearrange("(g p j) -> g p j", p=R, j=T)
        dst_rows = A["dst"][0:N_NODES].rearrange("(g p j) -> g p j", p=R, j=T)

        ident = sb("ident", [P, P])
        w_hi = sb("w_hi", [P, W_TOTAL], F32R)
        w_lo = sb("w_lo", [P, W_TOTAL], F32R)
        out_bias = sb("out_bias", [P, C], F32R)
        gate_sel = sb("gate_sel", [P, 2, P], F32R)
        ksum_h = sb("ksum_h", [P, CK, MIX_HEADS])
        den_sel = sb("den_sel", [P, CK, P], F32R)
        g_hi = sb("g_hi", [P, CK, C], F32R)
        g_lo = sb("g_lo", [P, CK, C], F32R)
        g2_bc = sb("g2_bc", [R, C])
        b2_bc = sb("b2_bc", [R, C])
        h_bias = sb("h_bias", [P, 4])
        s1_bias = sb("s1_bias", [P, 2])
        e1_bias = sb("e1_bias", [P, EXPERTS])
        s2_bias = sb("s2_bias", [P, 1])
        e2_bias = sb("e2_bias", [P, 2])
        beats = sb("beats", [R, EXPERTS, 2, EXPERTS])
        neg_half = sb("neg_half", [R, T])
        eps = sb("eps", [R, T])
        scale_rows = sb("scale_rows", [R, T, P])
        rs1 = [sb(f"rs1_{n}", [R, T]) for n in range(2)]
        xb = [sb(f"xb{n}", [R, T, C]) for n in range(2)]
        bn = [sb(f"bn_{n}", [R, T, 6]) for n in "xmyz"]
        mv = [sb(f"mv_{n}", [R, T, 2]) for n in "xmyzv"]
        rs = [sb(f"rs_{n}", [R, T]) for n in "xmyzv"]
        nm = [sb(f"nm_{n}", [R, T]) for n in "xmyzv"]
        veps = [sb(f"veps_{n}", [R, T]) for n in "xmyzv"]
        nmean = [sb(f"nmean_{n}", [R, T]) for n in "xmyzv"]
        LX, LM, LY, LZ = (0, 4), 1, 2, 3

        ctx0 = ExitStack()
        wk_raw = sb("wk_raw", [P, CK, C], stack=ctx0)
        wx_raw = sb("wx_raw", [P, CK, XA_W], stack=ctx0)
        attn_bc = sb("attn_bc", [P, 2, C], stack=ctx0)
        attn_prod = sb("attn_prod", [P, 2, CK, C], stack=ctx0)
        ctx0.close()
        row_n = sb("row_n", [R, T, C])
        xT_hi = sb("xT_hi", [P, CK, GR], F32R)
        xT_lo = sb("xT_lo", [P, CK, GR], F32R)
        qf = sb("qf", [P, CK, GR])
        idx = [sb(f"idx{n}", [R, 2, T], I32) for n in range(2)]

        ctx1 = ExitStack()
        w_raw = sb("w_raw", [P, W_TOTAL], stack=ctx1)
        wk_hi = sb("wk_hi", [P, CK, C], F32R, stack=ctx1)
        wk_lo = sb("wk_lo", [P, CK, C], F32R, stack=ctx1)
        wx_hi = sb("wx_hi", [P, CK, XA_W], F32R, stack=ctx1)
        wx_lo = sb("wx_lo", [P, CK, XA_W], F32R, stack=ctx1)
        wv = sb("wv", [P, CK, C], stack=ctx1)
        wm = sb("wm", [P, CK, C], stack=ctx1)
        g1_col = sb("g1_col", [P, CK], stack=ctx1)
        b1_col = sb("b1_col", [P, CK], stack=ctx1)
        ob_raw = sb("ob_raw", [P, C], stack=ctx1)
        ob_hi = sb("ob_hi", [P, C], F32R, stack=ctx1)
        w2_nmean = sb("w2_nmean", [P, 4], stack=ctx1)
        head_mask = sb("head_mask", [P, P], stack=ctx1)
        xn1 = [sb(f"xn1_{n}", [R, T, C], stack=ctx1) for n in range(2)]
        xr_hi = [sb(f"xr_hi{n}", [R, T, KX_W], F32R, stack=ctx1) for n in range(2)]
        xr_lo = [sb(f"xr_lo{n}", [R, T, KX_W], F32R, stack=ctx1) for n in range(2)]
        x1T_hi = [sb(f"x1T_hi{n}", [P, CK, GR], F32R, stack=ctx1) for n in range(2)]
        x1T_lo = [sb(f"x1T_lo{n}", [P, CK, GR], F32R, stack=ctx1) for n in range(2)]
        kf = sb("kf", [R, T, C], stack=ctx1)
        k_hi = [sb(f"k_hi{n}", [R, T, C], F32R, stack=ctx1) for n in range(2)]
        k_lo = [sb(f"k_lo{n}", [R, T, C], F32R, stack=ctx1) for n in range(2)]
        xts = [sb(f"xts{n}", [R, T, XA_W], stack=ctx1) for n in range(2)]
        kx = sb("kx", [P, CK, KX_W], stack=ctx1)
        kxT = sb("kxT", [P, CK, C], stack=ctx1)
        kvT = sb("kvT", [P, CK, P], stack=ctx1)
        ctx1.close()

        row_z = sb("row_z", [R, T, C])
        base = sb("base", [R, T, C])
        xmid = [sb(f"xmid{n}", [R, T, C]) for n in range(2)]
        rden = sb("rden", [R, T, MIX_HEADS])
        rden_hi = sb("rden_hi", [R, T, MIX_HEADS], F32R)
        scaleT = sb("scaleT", [P, GR], F32R)
        mT_hi = sb("mT_hi", [P, CK, GR], F32R)
        mT_lo = sb("mT_lo", [P, CK, GR], F32R)
        h_hi = sb("h_hi", [P, 4, GR], F32R)
        h_lo = sb("h_lo", [P, 4, GR], F32R)
        z_hi = sb("z_hi", [P, CK, GR], F32R)
        z_lo = sb("z_lo", [P, CK, GR], F32R)
        s1_hi = sb("s1_hi", [P, 2, GR], F32R)
        s1_lo = sb("s1_lo", [P, 2, GR], F32R)
        e1_hi = sb("e1_hi", [P, 4, GR], F32R)
        e1_lo = sb("e1_lo", [P, 4, GR], F32R)
        s2_hi = sb("s2_hi", [P, GR], F32R)
        s2_lo = sb("s2_lo", [P, GR], F32R)
        relu = [sb(f"relu{n}", [P, 2, GR]) for n in range(3)]
        gw_bc = sb("gw_bc", [R, C, EXPERTS])
        gb_bc = sb("gb_bc", [R, EXPERTS])
        logits = sb("logits", [R, T, EXPERTS])
        products = [sb(f"products{n}", [R, C]) for n in range(EXPERTS)]
        xg = [sb(f"xg{n}", [R, T, XT_W]) for n in range(2)]
        ag = [sb(f"ag{n}", [R, T, HEADS]) for n in range(2)]
        soft = sb("soft", [R, 2, T, 4])
        soft_s = sb("soft_s", [R, 2, T])
        cmpb = sb("cmpb", [R, T, EXPERTS, 2, EXPERTS])
        rank = sb("rank", [R, T, EXPERTS])
        top_e = sb("top_e", [R, T, EXPERTS])
        top_s = sb("top_s", [R, T])
        top_hi = sb("top_hi", [R, T, EXPERTS], F32R)
        gnn = sb("gnn", [R, T, HEAD_CH])

        psum = ctx.enter_context(nc.psum_tensor("psum", [P, 8, BANK], F32))

        def colT(b, n=None):
            return psum[:, b, 0:GR] if n is None else psum[:, b:b + n, 0:GR]

        def rowt(b, j):
            return psum[0:R, b + j // 2, (j % 2) * C:(j % 2 + 1) * C]

        def rows4(b):
            return psum[0:R, b:b + 2, :].rearrange("p b (j n) -> p (b j) n", j=2)

        def wslice(t, name, chunk, lo=0, n=None):
            at, cols = W_AT[name]
            at += chunk * cols + lo
            return t[:, at:at + (cols if n is None else n)]

        def split_mm(pe, out, w, x, first, last):
            (wh, wl), (xh, xl) = w, x
            pe.matmul(out, wh, xh, start=first, stop=False)
            pe.matmul(out, wh, xl, start=False, stop=False)
            return pe.matmul(out, wl, xh, start=False, stop=last)

        block = ctx.enter_context(nc.Block())

        def steps(eng, step, first, last):
            turns = (last - first) // 2
            with eng.Fori(first, first + 2 * turns, 2) as i:
                step(i, first % 2)
                step(i + 1, (first + 1) % 2)
            for i in range(first + 2 * turns, last):
                step(i, i % 2)

        def dma16(v, par):
            return 16 * (v // 2 + 1) if isinstance(v, int) else 8 * (v - par) + 16

        def load_idx(sp, v, par):
            sp.dma_start(idx[par][:, 0, :], src_rows[v]).then_inc(sem(f"idx{par}"), 16)
            sp.dma_start(idx[par][:, 1, :], dst_rows[v]).then_inc(sem(f"idx{par}"), 16)

        def wr(name, chunks):
            at, cols = W_AT[name]
            return w_raw[:, at:at + chunks * cols].rearrange("p (c n) -> p c n", c=chunks)

        def rows_of(name):
            return A[name].rearrange("(c p) n -> p c n", p=P)

        def column(name):
            return A[name].rearrange("(c p) -> p c", p=P)

        ew2 = W_AT["eW2"][0]
        ew2_raw = w_raw[:, ew2:ew2 + EXPERTS * P]
        ew2_halves = ew2_raw.rearrange("p (e m n) -> p e m n", e=EXPERTS, m=2)
        first_loads = [
            (wk_raw[:], rows_of("L0_mix_Wk")),
            (wx_raw[:, :, 0:C], rows_of("L0_gnn_weight")),
            (attn_bc[:, 0, :], A["L0_gnn_attn_r"].rearrange("h d -> (h d)").partition_broadcast(P)),
            (attn_bc[:, 1, :], A["L0_gnn_attn_l"].rearrange("h d -> (h d)").partition_broadcast(P)),
        ]
        later_loads = [
            (wr("Wq", 2), rows_of("L0_mix_Wq")), (wr("W1", 4), rows_of("L0_mix_W1")),
            (wr("W2", 4), rows_of("L0_mix_W2")), (wr("sW1", 2), rows_of("L0_ffn_sW1")),
            (wr("sW2", 2), rows_of("L0_ffn_sW2")), (wr("sW3", 1), rows_of("L0_ffn_sW3")),
            (wr("eW1", 8), A["L0_ffn_eW1"].rearrange("e (c p) n -> p (e c) n", p=P)),
            (wr("eW3", 2), A["L0_ffn_eW3"].rearrange("e g n -> (e g) n").rearrange("(q p) n -> p q n", p=P)),
            (wv[:], rows_of("L0_mix_Wv")), (wm[:], rows_of("L0_mix_Wm")),
            (g1_col[:], column("L0_mix_g1")), (b1_col[:], column("L0_mix_b1")),
            (s1_bias[:], column("L0_ffn_sb1")), (s2_bias[:], column("L0_ffn_sb2")),
            (e1_bias[:], A["L0_ffn_eb1"].rearrange("e p -> p e")),
            (e2_bias[:], A["L0_ffn_eb2"].rearrange("e g -> (e g)").rearrange("(q p) -> p q", p=P)),
            (g2_bc[:], A["L0_mix_g2"].partition_broadcast(R)), (b2_bc[:], A["L0_mix_b2"].partition_broadcast(R)),
        ]
        later_loads += [(ew2_halves[:, e, e % 2, :], A["L0_ffn_eW2"][e]) for e in range(EXPERTS)]
        for at in (0, 32, 64):
            later_loads.append((ob_raw[at:at + EXPERTS, :], A["L0_ffn_eb3"]))
            later_loads.append((ob_raw[at + EXPERTS:at + EXPERTS + 1, :],
                                A["L0_ffn_sb3"].rearrange("(o n) -> o n", o=1)))

        plain_parts = [(0, W_AT["W1"][0] + 2 * 512), (W_AT["sW1"][0], W_AT["eW1"][0] + 2 * 128),
                       (W_AT["eW1"][0] + 2 * 128, W_TOTAL)]

        def enter_phase2(eng):
            for name in ("p1_pe", "p1_act", "p1_dve", "p1_pool", "tables"):
                need(eng, name, 1)

        @block.sync
        def _(sp):
            def load_x(v, par, prefix):
                sp.dma_start(xb[par][:], x_rows[v]).then_inc(sem(f"{prefix}{par}"), 16)

            load_x(0, 0, "x")
            for to, of in first_loads:
                sp.dma_start(to, of).then_inc(sem("w_first"), 16)
            load_x(1, 1, "x")
            need(sp, "xn1", T)
            load_x(2, 0, "x")
            need(sp, "zeroed", 1)
            for to, of in later_loads:
                sp.dma_start(to, of, allow_slow_non_contiguous=True).then_inc(sem("w_later"), 16)

            def phase1(v, par):
                if not isinstance(v, int) or v + 3 < NG:
                    need(sp, "xn1", T * (v + 2))
                    load_x(v + 3, 1 - par, "x")
                elif v + 2 <= NG:
                    need(sp, "xn1", T * (v + 2))
                    load_x((v + 3) % 2, (v + 3) % 2, "y")
                    load_idx(sp, (v + 3) % 2, (v + 3) % 2)
                need(sp, "xts", 2 * (v + 1))
                sp.dma_start(xt_rows[v], xts[par][:, :, 0:XT_W]).then_inc(sem(f"tab{par}"), 16)
                sp.dma_start(al_rows[v], xts[par][:, :, XT_W:XA_W]).then_inc(sem(f"tab{par}"), 16)

            steps(sp, phase1, 0, NG - 5)
            for v in range(NG - 5, NG):
                phase1(v, v % 2)
            need(sp, "tab0", 32 * ((NG + 1) // 2))
            need(sp, "tab1", 32 * (NG // 2))
            sp.nop().then_inc(sem("tables"), 1)
            enter_phase2(sp)
            sp.dma_start(gw_bc[:], A["L0_ffn_gW"].partition_broadcast(R)).then_inc(sem("gw"), 16)
            sp.dma_start(gb_bc[:], A["L0_ffn_gb"].partition_broadcast(R)).then_inc(sem("gw"), 16)

            def phase2(i, par, a=True, c=True, more=True):
                if a and more:
                    need(sp, "gath", 128 * (i + 1))
                    load_idx(sp, i + 2, par)
                if c:
                    need(sp, "out", i - 1)
                    sp.dma_start(out_rows[i - 2], xmid[par][:]).then_inc(sem(f"st{par}"), 16)
                if a and more:
                    need(sp, "t", i + 1)
                    load_x(i + 2, par, "y")

            phase2(0, 0, c=False)
            phase2(1, 1, c=False)
            steps(sp, phase2, 2, NG - 2)
            for i in range(NG - 2, NG + 2):
                phase2(i, i % 2, a=i < NG, more=False)
            need(sp, "st0", 16 * ((NG + 1) // 2))
            need(sp, "st1", 16 * (NG // 2))

        @block.tensor
        def _(pe):
            def transposes(src, b, done, norm=None, before=0):
                for j in range(T):
                    if norm is not None:
                        need(pe, norm, before + j + 1)
                    for c in range(CK):
                        last = pe.transpose(psum[:, b + c, j * R:(j + 1) * R], src[:, j, c * P:(c + 1) * P],
                                            ident[0:R, 0:R])
                last.then_inc(sem(done), 1)

            def tile(t, c, j):
                return t[:, c, j * R:(j + 1) * R]

            def p1_transpose(v, par):
                need(pe, "x1T", v)
                transposes(xn1[par], 0, "x1t", "xn1", T * v)

            def p1_k(v, par):
                need(pe, "x1T", v + 1)
                need(pe, "kf", v)
                for j in range(T):
                    for c in range(CK):
                        last = split_mm(pe, rowt(2, j), (tile(x1T_hi[par], c, j), tile(x1T_lo[par], c, j)),
                                        (wk_hi[:, c, :], wk_lo[:, c, :]), c == 0, c == CK - 1)
                last.then_inc(sem("k_mm"), 1)

            def p1_table(v, par, pair):
                need(pe, "xts", 2 * v + pair)
                for j in (2 * pair, 2 * pair + 1):
                    for c in range(CK):
                        last = split_mm(pe, psum[0:R, 4 + j % 2, 0:XA_W],
                                        (tile(x1T_hi[par], c, j), tile(x1T_lo[par], c, j)),
                                        (wx_hi[:, c, :], wx_lo[:, c, :]), c == 0, c == CK - 1)
                last.then_inc(sem("xt_mm"), 1)

            def p1_kx(v, par, pair, first=False, last=False):
                if pair == 0:
                    need(pe, "k_split", v + 1)
                    need(pe, "x_split", v + 1)
                for j in (2 * pair, 2 * pair + 1):
                    for q in range(CK):
                        end = split_mm(pe, psum[:, 6 + q, 0:KX_W],
                                       (k_hi[par][:, j, q * P:(q + 1) * P], k_lo[par][:, j, q * P:(q + 1) * P]),
                                       (xr_hi[par][:, j, :], xr_lo[par][:, j, :]),
                                       first and j == 0, last and j == T - 1)
                if pair == 1:
                    end.then_inc(sem("kx"), 1)

            def phase1(v, par, kx=True, more=True):
                p1_k(v, par)
                if more:
                    p1_transpose(v + 1, 1 - par)
                for pair in range(2):
                    p1_table(v, par, pair)
                    if kx:
                        p1_kx(v - 1, 1 - par, pair, first=isinstance(v, int) and v == 1)

            def hidden(name, chunk, o, b, x, n=CK):
                for c in range(n):
                    last = split_mm(pe, colT(b), (wslice(w_hi, name, chunk + c, o * P, P),
                                                  wslice(w_lo, name, chunk + c, o * P, P)),
                                    (x[0][:, c, :], x[1][:, c, :]), c == 0, c == n - 1)
                return last

            def p2_transpose_x(i):
                transposes(row_n, 2, "xt2", "x_norm", T * i)

            def p2_q(i):
                need(pe, "xT", i + 1)
                for q in range(CK):
                    last = hidden("Wq", 0, q, 6 + q, (xT_hi, xT_lo))
                last.then_inc(sem("q_mm"), 1)

            def p2_den(i):
                need(pe, "q", i + 1)
                for j in range(T):
                    for q in range(CK):
                        last = pe.matmul(psum[0:R, 6, j * MIX_HEADS:(j + 1) * MIX_HEADS], tile(qf, q, j),
                                         ksum_h[:, q, :], start=q == 0, stop=q == CK - 1)
                last.then_inc(sem("den"), 1)

            need(pe, "ident", 1)
            p1_transpose(0, 0)
            need(pe, "w_split1", 1)
            phase1(0, 0, kx=False)
            phase1(1, 1)
            steps(pe, phase1, 2, NG - 1)
            phase1(NG - 1, (NG - 1) % 2, more=False)
            need(pe, "w_later", 16 * len(later_loads))
            for o in range(4):
                for c in range(CK):
                    last = pe.matmul(psum[:, 0, o:o + 1], wslice(w_raw, "W1", 2 + c, o * P, P), b1_col[:, c:c + 1],
                                     start=c == 0, stop=c == CK - 1)
            last.then_inc(sem("hb_mm"), 1)
            for pair in range(2):
                p1_kx(NG - 1, (NG - 1) % 2, pair, last=True)

            p2_transpose_x(0)
            need(pe, "kxs", 1)
            need(pe, "xts", 2 * NG)
            for c in range(CK):
                for q in range(CK):
                    last = pe.transpose(psum[:, 4 + c, q * P:(q + 1) * P], kx[:, q, c * P:(c + 1) * P], ident[:])
            last.then_inc(sem("kxt_mm"), 1)
            need(pe, "kxT", 1)
            for q in range(CK):
                for c in range(CK):
                    last = pe.matmul(psum[:, 1, q * P:(q + 1) * P], wv[:, c, q * P:(q + 1) * P],
                                     kxT[:, c, q * P:(q + 1) * P], start=c == 0, stop=c == CK - 1)
            last.then_inc(sem("kv_mm"), 1)
            need(pe, "w_lo", 2)
            p2_q(0)
            need(pe, "kvT", 1)
            for q in range(CK):
                last = pe.matmul(psum[:, 5, q * C:(q + 1) * C], kvT[:, q, :], wm[:, q, :], start=True, stop=True)
            last.then_inc(sem("p1_pe"), 1)

            def w1_part(half, o, b, x):
                for c in range(CK):
                    k = 2 * half + c
                    last = split_mm(pe, colT(b), (wslice(w_hi, "W1", k, o * P, P), wslice(w_lo, "W1", k, o * P, P)),
                                    (x[0][:, c, :], x[1][:, c, :]), k == 0, k == 3)
                return last

            def w2_pair(i, pair, c):
                if pair == 0:
                    need(pe, "h_lo", 2 * i)
                if c:
                    need(pe, *(("s1_relu", 2 * (i - 1)), ("e1_relu", 4 * (i - 2) + 1))[pair])
                for j in (2 * pair, 2 * pair + 1):
                    for k in range(4):
                        last = split_mm(pe, rowt(0, j), (tile(h_hi, k, j), tile(h_lo, k, j)),
                                        (wslice(w_hi, "W2", k), wslice(w_lo, "W2", k)), k == 0, k == 3)
                last.then_inc(sem("w2"), 1)

            def phase2(i, par, a=True, b=True, c=True, started=False):
                xT, mT, zT = (xT_hi, xT_lo), (mT_hi, mT_lo), (z_hi, z_lo)

                def transpose_scales():
                    if c:
                        need(pe, "gate_rows", i - 1)
                    if a:
                        need(pe, "den_rows", i + 1)
                    elif b:
                        need(pe, "h_relu", 4 * (i - 1) + 4)
                    for j in range(T):
                        last = pe.transpose(psum[:, 7, j * R:(j + 1) * R], scale_rows[:, j, :], ident[0:R, 0:R])
                    last.then_inc(sem("scale_t"), 1)

                def hidden_of_xn():
                    w1_part(0, 0, 4, xT)
                    w1_part(0, 1, 5, xT)

                if b:
                    need(pe, "y", i - 1)
                    transposes(row_n, 0, "mt", "m_norm", T * (i - 1))
                    w1_part(0, 2, 6, xT)
                    w1_part(0, 3, 7, xT)
                    need(pe, "mT", i)
                    for o in range(2):
                        w1_part(1, o, 4 + o, mT).then_inc(sem("h_mm"), 1)
                if c:
                    if not b:
                        need(pe, "y", i - 1)
                    transposes(row_z, 0, "zt", "z_norm", T * (i - 2))
                if b:
                    for o in range(2, 4):
                        w1_part(1, o, 4 + o, mT).then_inc(sem("h_mm"), 1)
                if a and not started:
                    need(pe, "out", i - 2)
                    p2_transpose_x(i)
                if c:
                    need(pe, "zT", i - 1)
                    if b:
                        need(pe, "h_relu", 4 * (i - 1) + 2)
                    else:
                        need(pe, "e2g", 2 * (i - 2))
                    hidden("sW1", 0, 0, 5, zT).then_inc(sem("s1_mm"), 1)
                    hidden("sW1", 0, 1, 0, zT).then_inc(sem("s1_mm"), 1)
                if a and not started:
                    if b:
                        need(pe, "h_relu", 4 * (i - 1) + 4)
                    p2_q(i)
                if c:
                    if not a:
                        need(pe, "out", i - 2)
                    for e in range(EXPERTS):
                        hidden("eW1", 2 * e, 0, 1 + e, zT).then_inc(sem("e1_mm"), 1)
                if b and not c:
                    w2_pair(i, 0, c)
                if a and not started:
                    p2_den(i)
                if b:
                    for pair in range(2) if c else (1,):
                        w2_pair(i, pair, c)
                if a:
                    transpose_scales()
                if c:
                    need(pe, "s1_lo", i - 1)
                    need(pe, "e1_relu", 4 * (i - 1))
                    hidden("sW2", 0, 0, 4, (s1_hi, s1_lo)).then_inc(sem("s2_mm"), 1)
                if a:
                    need(pe, "scaleT", i + 1)
                    for q in range(CK):
                        last = pe.matmul(colT(6 + q), den_sel[:, q, :], scaleT[:], start=True, stop=True)
                    last.then_inc(sem("dx"), 1)
                if c:
                    for q in range(2):
                        need(pe, "e1_lo", 2 * (i - 2) + q + 1)
                        for m in range(2):
                            e = 2 * q + m
                            last = split_mm(pe, colT(2 + q), (wslice(w_hi, "eW2", e), wslice(w_lo, "eW2", e)),
                                            (e1_hi[:, e, :], e1_lo[:, e, :]), m == 0, m == 1)
                        last.then_inc(sem("e2_mm"), 1)
                    if not a:
                        transpose_scales()
                    need(pe, "scaleT", i + 1)
                    need(pe, "s2_relu", i - 1)
                    for q in range(2):
                        last = pe.matmul(colT(4 + q), gate_sel[:, q, :], scaleT[:], start=True, stop=True)
                    last.then_inc(sem("gb"), 1)
                if a:
                    if not c:
                        if b:
                            need(pe, "h_relu", 4 * (i - 1) + 2)
                        hidden_of_xn()
                    need(pe, "qz", i + 1)
                    for j in range(T):
                        for q in range(CK):
                            last = split_mm(pe, rowt(6, j), (tile(z_hi, q, j), tile(z_lo, q, j)),
                                            (g_hi[:, q, :], g_lo[:, q, :]), q == 0, q == CK - 1)
                        if j % 2:
                            last.then_inc(sem("m_mm"), 1)
                    if c:
                        need(pe, "e2g", 2 * (i - 1))
                        hidden_of_xn()
                if c:
                    need(pe, "s2_lo", i - 1)
                    need(pe, "e2_relu", 2 * (i - 1))
                    for j in range(T):
                        out = rowt(2, j)
                        pe.matmul(out, scaleT[:, j * R:(j + 1) * R], out_bias[:], start=True, stop=False)
                        split_mm(pe, out, (s2_hi[:, j * R:(j + 1) * R], s2_lo[:, j * R:(j + 1) * R]),
                                 (wslice(w_hi, "sW3", 0), wslice(w_lo, "sW3", 0)), False, False)
                        if j == 0:
                            need(pe, "e2_lo", i - 1)
                        for q in range(2):
                            last = split_mm(pe, out, (tile(h_hi, q, j), tile(h_lo, q, j)),
                                            (wslice(w_hi, "eW3", q), wslice(w_lo, "eW3", q)), False, q == 1)
                    last.then_inc(sem("out_mm"), 1)

            p2_den(0)
            need(pe, "g_split", 1)
            phase2(0, 0, b=False, c=False, started=True)
            phase2(1, 1, c=False)
            phase2(2, 0)
            steps(pe, phase2, 3, NG)
            phase2(NG, NG % 2, a=False)
            phase2(NG + 1, (NG + 1) % 2, a=False, b=False)

        @block.scalar
        def _(act):
            def normalize(out, src, which, done):
                for j in range(T):
                    act.activation(out[:, j, :], src(j), ACT.Identity, bias=nm[which][:, j:j + 1],
                                   scale=rs[which][:, j:j + 1]).then_inc(sem(done), 1)

            def p1_norm(v, par):
                need(act, "rs_x1", v + 1)
                need(act, "x1t", v - 1)
                need(act, "x_split", v - 1)
                normalize(xn1[par], lambda j: xb[par][:, j, :], LX[par], "xn1")

            def p1_copyT(v, par):
                need(act, "x1t", v + 1)
                need(act, "xt_mm", 2 * (v - 1))
                act.activation(x1T_hi[par][:], colT(0, 2), ACT.Copy).then_inc(sem("x1T_hi"), 1)

            def phase1(v, par, more=2):
                need(act, "k_mm", v + 1)
                need(act, "k_split", v)
                act.activation(kf[:], rows4(2), ACT.Exp).then_inc(sem("k_exp"), 1)
                if more >= 1:
                    p1_copyT(v + 1, 1 - par)
                for pair in range(2):
                    need(act, "xt_mm", 2 * v + pair + 1)
                    if pair == 0:
                        need(act, f"tab{par}", 2 * dma16(v - 2, par))
                    act.activation(xts[par][:, 2 * pair:2 * pair + 2, :], psum[0:R, 4:6, 0:XA_W],
                                   ACT.Copy).then_inc(sem("xts"), 1)
                if more >= 2:
                    p1_norm(v + 2, par)

            p1_norm(0, 0)
            p1_copyT(0, 0)
            p1_norm(1, 1)
            phase1(0, 0)
            phase1(1, 1)
            steps(act, phase1, 2, NG - 3)
            need(act, "w_later", 16 * len(later_loads))
            for v in range(NG - 3, NG):
                phase1(v, v % 2, more=NG - 1 - v)
                if v == NG - 2:
                    need(act, "w2_mean", 1)
                    for k in range(4):
                        act.activation(wslice(w_hi, "W2", k), wslice(w_raw, "W2", k), ACT.Identity,
                                       bias=w2_nmean[:, k:k + 1])
                if v == NG - 1:
                    for c in range(CK):
                        act.activation(wslice(w_hi, "W1", 2 + c), wslice(w_raw, "W1", 2 + c), ACT.Identity,
                                       scale=g1_col[:, c:c + 1])
                lo, hi = plain_parts[v - (NG - 3)]
                act.activation(w_hi[:, lo:hi], w_raw[:, lo:hi], ACT.Copy).then_inc(sem("w_hi"), 1)

            def p2_norm_x(i, par):
                need(act, "rs_x", i + 1)
                normalize(row_n, lambda j: xb[par][:, j, :], LX[par], "x_norm")

            def p2_copy_xT(i):
                need(act, "xt2", i + 1)
                act.activation(xT_hi[:], colT(2, 2), ACT.Copy).then_inc(sem("xT_hi"), 1)

            def p2_exp(i):
                need(act, "q_mm", i + 1)
                need(act, "qz", i)
                act.activation(qf[:], colT(6, 2), ACT.Exp).then_inc(sem("q_exp"), 1)

            p2_norm_x(0, 0)
            p2_copy_xT(0)
            need(act, "kxt_mm", 1)
            act.activation(kxT[:], psum[:, 4:6, 0:C], ACT.Copy).then_inc(sem("kxT"), 1)
            p2_exp(0)
            need(act, "p1_pe", 1)
            act.activation(g_hi[:], psum[:, 5, :].rearrange("p (q n) -> p q n", q=CK),
                           ACT.Copy).then_inc(sem("g_hi"), 1)
            act.drain().then_inc(sem("p1_act"), 1)

            def relu_split(out, hi, b, bias, count, mm, done):
                need(act, mm, count)
                act.activation(out, colT(b), ACT.Relu, bias=bias)
                act.activation(hi, colT(b), ACT.Relu, bias=bias).then_inc(sem(done), 1)

            def copy_scales(i):
                need(act, "scale_t", i + 1)
                act.activation(scaleT[:], colT(7), ACT.Copy).then_inc(sem("scaleT"), 1)

            def soft_exp(i, a, c):
                need(act, "soft_sub", i + 1)
                part = soft[:, 0 if c else 1:2 if a else 1, :, :]
                act.activation(part, part, ACT.Exp).then_inc(sem("soft_exp"), 1)

            def phase2(i, par, a=True, b=True, c=True, started=False):
                if b:
                    need(act, "mt", i)
                    act.activation(mT_hi[:], colT(0, 2), ACT.Copy).then_inc(sem("mT_hi"), 1)
                if a and not started:
                    if b:
                        need(act, "mt", i)
                    p2_norm_x(i, par)
                if c:
                    need(act, "rs_z", i - 1)
                    need(act, "zt", i - 2)
                    normalize(row_z, lambda j: xmid[par][:, j, :], LZ, "z_norm")
                if b:
                    need(act, "e2_lo", i - 2)
                for o in range(2):
                    if b:
                        relu_split(relu[0][:, o, :], h_hi[:, o, :], 4 + o, h_bias[:, o:o + 1],
                                   4 * (i - 1) + o + 1, "h_mm", "h_relu")
                    if c and o == 0:
                        need(act, "zt", i - 1)
                        act.activation(z_hi[:], colT(0, 2), ACT.Copy).then_inc(sem("z_hi"), 1)
                if b:
                    need(act, "e1_lo", 2 * (i - 2))
                    for o in range(2, 4):
                        relu_split(relu[1][:, o - 2, :], h_hi[:, o, :], 4 + o, h_bias[:, o:o + 1],
                                   4 * (i - 1) + o + 1, "h_mm", "h_relu")
                        if o == 2 and a:
                            p2_copy_xT(i)
                elif a and not started:
                    p2_copy_xT(i)
                if c:
                    need(act, "s2_lo", i - 2)
                    for o in range(2):
                        relu_split(relu[2][:, o, :], s1_hi[:, o, :], 5 if o == 0 else 0, s1_bias[:, o:o + 1],
                                   2 * (i - 2) + o + 1, "s1_mm", "s1_relu")
                if a and not started:
                    p2_exp(i)
                if c:
                    for e in range(EXPERTS):
                        if e == 0:
                            need(act, *(("h_lo", 2 * (i - 1) + 1) if b else ("e2_lo", i - 2)))
                        if e == 2:
                            need(act, *(("h_lo", 2 * (i - 1) + 2) if b else ("e1_lo", 2 * (i - 2))))
                        relu_split(relu[e // 2][:, e % 2, :], e1_hi[:, e, :], 1 + e, e1_bias[:, e:e + 1],
                                   4 * (i - 2) + e + 1, "e1_mm", "e1_relu")
                        if e == 2:
                            soft_exp(i, a, c)
                    need(act, "gates", i - 1)
                    act.activation(top_e[:], soft[:, 0, :, :], ACT.Exp).then_inc(sem("top_exp"), 1)
                if a:
                    copy_scales(i)
                if c:
                    need(act, "s1_lo", i - 1)
                    relu_split(relu[2][:, 0, :], s2_hi[:], 4, s2_bias[:, 0:1], i - 1, "s2_mm", "s2_relu")
                if a:
                    for q in range(CK):
                        need(act, "q_den", 2 * i + q + 1)
                        act.activation(z_hi[:, q, :], qf[:, q, :], ACT.Copy).then_inc(sem("qz_hi"), 1)
                if c:
                    need(act, "e1_lo", 2 * (i - 2) + 1)
                    for q in range(2):
                        need(act, "e2_mm", 2 * (i - 2) + q + 1)
                        act.activation(relu[0][:, q, :], colT(2 + q), ACT.Relu,
                                       bias=e2_bias[:, q:q + 1]).then_inc(sem("e2_relu"), 1)
                    if not a:
                        copy_scales(i)
                    for q in range(2):
                        need(act, "e2g", 2 * (i - 2) + q + 1)
                        act.activation(h_hi[:, q, :], relu[0][:, q, :], ACT.Copy).then_inc(sem("e2_hi"), 1)
                if a:
                    need(act, "rs_m", i + 1)
                    need(act, "xt2", i + 1)
                    normalize(row_n, lambda j: rowt(6, j), LM, "m_norm")
                if a and not c:
                    soft_exp(i, a, c)

            enter_phase2(act)
            phase2(0, 0, b=False, c=False, started=True)
            phase2(1, 1, c=False)
            phase2(2, 0)
            steps(act, phase2, 3, NG)
            phase2(NG, NG % 2, a=False)
            phase2(NG + 1, (NG + 1) % 2, a=False, b=False)

        @block.vector
        def _(dve):
            tt, ts, stt = dve.tensor_tensor, dve.tensor_scalar, dve.scalar_tensor_tensor

            def stats(which, tiles, src):
                for j in tiles:
                    dve.bn_stats(bn[which % 4][:, j, :], src(j))

            def aggregate(which, done):
                dve.drain()
                for j in range(T):
                    last = dve.bn_aggr(mv[which][:, j, :], bn[which % 4][:, j, :])
                last.then_inc(sem(done), 1)

            def p1_stats(v, par):
                dve.drain()
                need(dve, f"x{par}", dma16(v, par))
                need(dve, "rs_x1", v - 1)
                stats(LX[par], range(T), lambda j: xb[par][:, j, :])
                aggregate(LX[par], "mv_x1")

            p1_stats(0, 0)
            need(dve, "w_first", 16 * len(first_loads))
            dve.tensor_copy(wk_hi[:], wk_raw[:])
            for s in range(2):
                tt(attn_prod[:, s, :, :], wx_raw[:, :, 0:C],
                   attn_bc[:, s, :].unsqueeze(1).broadcast_to([P, CK, C]), ALU.mult)
            dve.drain()
            tt(wk_lo[:], wk_raw[:], wk_hi[:], ALU.subtract)
            for s in range(2):
                dve.reduce_sum(wx_raw[:, :, C + HEADS * s:C + HEADS * (s + 1)],
                               attn_prod[:, s, :, :].rearrange("p c (h d) -> p c h d", h=HEADS), AXX)
            dve.drain()
            dve.tensor_copy(wx_hi[:], wx_raw[:])
            dve.drain()
            tt(wx_lo[:], wx_raw[:], wx_hi[:], ALU.subtract).then_inc(sem("w_split1"), 1)

            def p1_lowT(v, par):
                need(dve, "x1T_hi", v + 1)
                tt(x1T_lo[par][:], colT(0, 2), x1T_hi[par][:], ALU.subtract).then_inc(sem("x1T"), 1)

            def phase1(v, par, more=2):
                if more >= 2:
                    p1_stats(v + 2, par)
                need(dve, "kx", v - 1)
                need(dve, "xn1", T * (v + 1))
                if isinstance(v, int) and v < 2:
                    need(dve, "xr_ones", 1)
                dve.tensor_copy(xr_hi[par][:, :, 0:C], xn1[par][:]).then_inc(sem("xr_hi"), 1)
                need(dve, "k_exp", v + 1)
                ts(kf[:], kf[:], 1.0, None, ALU.min)
                if more >= 1:
                    p1_lowT(v + 1, 1 - par)
                dve.drain()
                stt(kf[:], rows4(2), 1.0, kf[:], ALU.add, ALU.max).then_inc(sem("kf"), 1)
                dve.drain()
                dve.tensor_copy(k_hi[par][:], kf[:]).then_inc(sem("k_hi"), 1)

            p1_lowT(0, 0)
            p1_stats(1, 1)
            phase1(0, 0)
            phase1(1, 1)
            steps(dve, phase1, 2, NG - 3)

            w2 = w_raw[:, W_AT["W2"][0]:W_AT["W2"][0] + 4 * C].rearrange("p (k n) -> p k n", k=4)

            def small_constants():
                dve.memset(head_mask[:], 0.0)
                dve.memset(ksum_h[:], 0.0)
                dve.drain()
                for h in range(P // MIX_CH):
                    dve.memset(head_mask[h * MIX_CH:(h + 1) * MIX_CH, h * MIX_CH:(h + 1) * MIX_CH], 1.0)
                need(dve, "w_later", 16 * len(later_loads))
                for e in range(EXPERTS):
                    tt(gate_sel[:, e // 2, e % 2 * HEAD_CH:(e % 2 + 1) * HEAD_CH],
                       ident[:, e:e + 1].broadcast_to([P, HEAD_CH]),
                       ident[:, 32 + e:33 + e].broadcast_to([P, HEAD_CH]), ALU.add)
                per = MIX_HEADS // CK
                for h in range(MIX_HEADS):
                    tt(den_sel[:, h // per, h % per * MIX_CH:(h % per + 1) * MIX_CH],
                       ident[:, 8 + h:9 + h].broadcast_to([P, MIX_CH]),
                       ident[:, 40 + h:41 + h].broadcast_to([P, MIX_CH]), ALU.add)
                need(dve, "zeroed", 1)
                for at in (0, 32):
                    dve.tensor_copy(out_bias[at:at + EXPERTS + 1, :], ob_raw[at:at + EXPERTS + 1, :])
                dve.tensor_copy(ob_hi[64:64 + EXPERTS + 1, :], ob_raw[64:64 + EXPERTS + 1, :])
                dve.reduce_sum(w2_nmean[:], w2, AXX)
                dve.drain()
                ts(w2_nmean[:], w2_nmean[:], -1.0 / C, None, ALU.mult).then_inc(sem("w2_mean"), 1)
                tt(out_bias[64:64 + EXPERTS + 1, :], ob_raw[64:64 + EXPERTS + 1, :], ob_hi[64:64 + EXPERTS + 1, :],
                   ALU.subtract)

            def second_parts(n):
                need(dve, "w_hi", n + 1)
                lo, hi = plain_parts[n]
                tt(w_lo[:, lo:hi], w_raw[:, lo:hi], w_hi[:, lo:hi], ALU.subtract).then_inc(sem("w_lo"), 1)
                if n == 1:
                    for k in range(4):
                        stt(wslice(w_lo, "W2", k), wslice(w_raw, "W2", k), w2_nmean[:, k:k + 1],
                            wslice(w_hi, "W2", k), ALU.add, ALU.subtract)

            def x_stats(v, par):
                need(dve, f"y{par}", dma16(v, par))
                need(dve, "rs_x", v - 1)
                stats(LX[par], range(T), lambda j: xb[par][:, j, :])
                aggregate(LX[par], "mv_x")

            def p2_lowT(i):
                need(dve, "xT_hi", i + 1)
                tt(xT_lo[:], colT(2, 2), xT_hi[:], ALU.subtract).then_inc(sem("xT"), 1)

            def p2_feature(i):
                need(dve, "q_exp", i + 1)
                ts(qf[:], qf[:], 1.0, None, ALU.min)
                dve.drain()
                stt(qf[:], colT(6, 2), 1.0, qf[:], ALU.add, ALU.max).then_inc(sem("q"), 1)

            for v in range(NG - 3, NG):
                if v == NG - 1:
                    need(dve, "rs_x1", NG)
                    x_stats(0, 0)
                phase1(v, v % 2, more=NG - 1 - v)
                if v == NG - 3:
                    small_constants()
                else:
                    second_parts(v - (NG - 3) - 1)

            second_parts(2)
            need(dve, "kx", NG)
            dve.tensor_copy(kx[:], psum[:, 6:8, 0:KX_W]).then_inc(sem("kxs"), 1)
            for c in range(CK):
                stt(wslice(w_lo, "W1", 2 + c), wslice(w_raw, "W1", 2 + c), g1_col[:, c:c + 1],
                    wslice(w_hi, "W1", 2 + c), ALU.mult, ALU.subtract)
            p2_lowT(0)
            need(dve, "hb_mm", 1)
            dve.tensor_copy(h_bias[:], psum[:, 0, 0:4])
            dve.drain()
            per = MIX_HEADS // CK
            for q in range(CK):
                ts(ksum_h[:, q, q * per:(q + 1) * per], head_mask[:, 0:P:MIX_CH], kx[:, q, C:C + 1], None, ALU.mult)
            need(dve, "kv_mm", 1)
            for q in range(CK):
                last = tt(kvT[:, q, :], psum[:, 1, q * P:(q + 1) * P], head_mask[:], ALU.mult)
            last.then_inc(sem("kvT"), 1)
            p2_feature(0)
            need(dve, "g_hi", 1)
            tt(g_lo[:], psum[:, 5, :].rearrange("p (q n) -> p q n", q=CK), g_hi[:],
               ALU.subtract).then_inc(sem("g_split"), 1)
            dve.drain().then_inc(sem("p1_dve"), 1)

            def expert_logits(tiles):
                for j in tiles:
                    for e in range(EXPERTS):
                        dve.tensor_tensor_reduce(out=products[e][:], in0=row_z[:, j, :], in1=gw_bc[:, :, e],
                                                 scale=1.0, scalar=0.0, op0=ALU.mult, op1=ALU.add,
                                                 accum_out=logits[:, j, e:e + 1])
                    dve.drain()

            def soft_chain_in(i, par, a, c):
                if a:
                    need(dve, "gath", 128 * (i + 1))
                    tt(soft[:, 1, :, :], ag[par][:], xg[par][:, :, C:C + HEADS], ALU.add)
                    dve.drain()
                if c:
                    tt(soft[:, 0, :, :], logits[:], gb_bc[:].unsqueeze(1).broadcast_to([R, T, EXPERTS]), ALU.add)
                if a:
                    stt(soft[:, 1, :, :], soft[:, 1, :, :], 0.01, soft[:, 1, :, :], ALU.mult, ALU.max)
                s, m = soft_views(a, c)
                dve.drain()
                dve.reduce_max(m, s, AXX)
                dve.drain()
                tt(s, s, m.unsqueeze(3).broadcast_to(s.shape), ALU.subtract).then_inc(sem("soft_sub"), 1)

            def soft_views(a, c):
                lo, hi = (0 if c else 1), (2 if a else 1)
                return soft[:, lo:hi, :, :], soft_s[:, lo:hi, :]

            def soft_chain_out(i, a, c):
                s, m = soft_views(a, c)
                need(dve, "soft_exp", i + 1)
                dve.reduce_sum(m, s, AXX)
                dve.drain()
                dve.reciprocal(m, m)
                dve.drain()
                last = tt(s, s, m.unsqueeze(3).broadcast_to(s.shape), ALU.mult)
                if c:
                    last.then_inc(sem("gates"), 1)
                dve.drain()

            def compare(i):
                g = soft[:, 0, :, :]
                for n, op in enumerate((ALU.is_ge, ALU.is_gt)):
                    tt(cmpb[:, :, :, n, :], g.unsqueeze(2).broadcast_to([R, T, EXPERTS, EXPERTS]),
                       g.unsqueeze(3).broadcast_to([R, T, EXPERTS, EXPERTS]), op)
                dve.drain()
                cm = cmpb[:].rearrange("p t e n j -> p t (e n j)")
                tt(cm, cm, beats[:].rearrange("p e n j -> p (e n j)").unsqueeze(1).broadcast_to(
                    [R, T, 2 * EXPERTS * EXPERTS]), ALU.mult)
                dve.drain()
                dve.reduce_sum(rank[:], cmpb[:].rearrange("p t e n j -> p t e (n j)"), AXX)

            def top_weights(i):
                dve.drain()
                need(dve, "top_exp", i - 1)
                need(dve, "scale_t", i)
                stt(top_e[:], rank[:], float(TOPK), top_e[:], ALU.is_lt, ALU.mult)
                dve.drain()
                dve.reduce_sum(top_s[:], top_e[:], AXX)
                dve.drain()
                dve.reciprocal(top_s[:], top_s[:])
                dve.drain()
                tt(top_e[:], top_e[:], top_s[:].unsqueeze(2).broadcast_to([R, T, EXPERTS]), ALU.mult)
                dve.drain()
                dve.tensor_copy(top_hi[:], top_e[:])
                dve.drain()
                for at in (0, 64):
                    dve.tensor_copy(scale_rows[:, :, at:at + EXPERTS], top_hi[:])
                tt(scale_rows[:, :, 32:32 + EXPERTS], top_e[:], top_hi[:], ALU.subtract).then_inc(sem("gate_rows"), 1)

            def one_over_den(i):
                need(dve, "den", i + 1)
                ts(rden[:], psum[0:R, 6, 0:T * MIX_HEADS].rearrange("p (j h) -> p j h", j=T), ATT_EPS, None, ALU.add)
                dve.drain()
                dve.reciprocal(rden[:], rden[:])
                dve.drain()
                dve.tensor_copy(rden_hi[:], rden[:])
                dve.drain()
                dve.tensor_copy(scale_rows[:, :, 8:8 + MIX_HEADS], rden_hi[:])
                tt(scale_rows[:, :, 40:40 + MIX_HEADS], rden[:], rden_hi[:], ALU.subtract).then_inc(sem("den_rows"), 1)

            def y_stats_end(i):
                need(dve, "w2", 2 * i)
                stats(LY, (2, 3), lambda j: rowt(0, j))
                aggregate(LY, "mv_y")

            def residual(v, par, tiles):
                for j in tiles:
                    last = stt(base[:, j, :], xb[par][:, j, :], rs1[par][:, j:j + 1], b2_bc[:], ALU.mult, ALU.add)
                if T - 1 in tiles:
                    last.then_inc(sem("t"), 1)

            def graph_layer(v, par):
                dve.drain()
                need(dve, "base", v)
                for h in range(HEADS):
                    for j in range(T):
                        part = xg[par][:, j, h * HEAD_CH:(h + 1) * HEAD_CH]
                        al = soft[:, 1, j, h:h + 1]
                        if h == 0:
                            last = ts(gnn[:, j, :], part, al, nm[LX[par]][:, j:j + 1], ALU.mult, ALU.add)
                        else:
                            last = stt(gnn[:, j, :], part, al, gnn[:, j, :], ALU.mult, ALU.add)
                    if h == HEADS - 1:
                        last.then_inc(sem("gnn"), 1)
                    dve.drain()

            def phase2(i, par, a=True, b=True, c=True, more=True, started=False):
                if b:
                    residual(i - 1, 1 - par, (0,))
                    need(dve, "mT_hi", i)
                    tt(mT_lo[:], colT(0, 2), mT_hi[:], ALU.subtract).then_inc(sem("mT"), 1)
                    graph_layer(i - 1, 1 - par)
                if c:
                    need(dve, "z_hi", i - 1)
                    tt(z_lo[:], colT(0, 2), z_hi[:], ALU.subtract).then_inc(sem("zT"), 1)
                if b:
                    residual(i - 1, 1 - par, (1, 2, 3))
                if a and not started:
                    p2_lowT(i)
                if c:
                    expert_logits((0, 1, 2))
                if a and not started:
                    p2_feature(i)
                if c:
                    expert_logits((3,))
                    soft_chain_in(i, par, a, c)
                    soft_chain_out(i, a, c)
                    compare(i)
                    top_weights(i)
                if a:
                    one_over_den(i)
                if a and more:
                    x_stats(i + 1, 1 - par)
                if b:
                    need(dve, "w2", 2 * i - 1)
                    need(dve, "rs_y", i - 1)
                    stats(LY, (0, 1), lambda j: rowt(0, j))
                if b and not c:
                    y_stats_end(i)
                if a:
                    need(dve, "dx", i + 1)
                    for q in range(CK):
                        tt(qf[:, q, :], qf[:, q, :], colT(6 + q), ALU.mult).then_inc(sem("q_den"), 1)
                    for q in range(CK):
                        need(dve, "qz_hi", 2 * i + q + 1)
                        last = tt(z_lo[:, q, :], qf[:, q, :], z_hi[:, q, :], ALU.subtract)
                    last.then_inc(sem("qz"), 1)
                if b and c:
                    y_stats_end(i)
                if c:
                    need(dve, "e2_relu", 2 * (i - 1))
                    need(dve, "gb", i - 1)
                    for q in range(2):
                        tt(relu[0][:, q, :], relu[0][:, q, :], colT(4 + q), ALU.mult).then_inc(sem("e2g"), 1)
                if a:
                    need(dve, "rs_m", i)
                    for pair in range(2):
                        need(dve, "m_mm", 2 * i + pair + 1)
                        stats(LM, (2 * pair, 2 * pair + 1), lambda j: rowt(6, j))
                    aggregate(LM, "mv_m")
                if c:
                    for q in range(2):
                        need(dve, "e2_hi", 2 * (i - 2) + q + 1)
                        last = tt(h_lo[:, q, :], relu[0][:, q, :], h_hi[:, q, :], ALU.subtract)
                    last.then_inc(sem("e2_lo"), 1)
                if b:
                    need(dve, "rs_y", i)
                    need(dve, f"st{1 - par}", dma16(i - 3, 1 - par))
                    for j in range(T):
                        last = stt(xmid[1 - par][:, j, :], rowt(0, j), rs[LY][:, j:j + 1], g2_bc[:],
                                   ALU.mult, ALU.mult)
                    last.then_inc(sem("y"), 1)
                    dve.drain()
                    need(dve, "base", i)
                    tt(xmid[1 - par][:], xmid[1 - par][:], base[:], ALU.add).then_inc(sem("xmid"), 1)
                    dve.drain()
                    need(dve, "rs_z", i - 1)
                    stats(LZ, range(T), lambda j: xmid[1 - par][:, j, :])
                    aggregate(LZ, "mv_z")
                if a and not c:
                    dve.drain()
                    soft_chain_in(i, par, a, c)
                    soft_chain_out(i, a, c)
                if c:
                    need(dve, "out_mm", i - 1)
                    tt(xmid[par][:], xmid[par][:], rows4(2), ALU.add).then_inc(sem("out"), 1)

            enter_phase2(dve)
            need(dve, "masks", 1)
            phase2(0, 0, b=False, c=False, started=True)
            phase2(1, 1, c=False)
            need(dve, "gw", 32)
            phase2(2, 0)
            steps(dve, phase2, 3, NG - 1)
            phase2(NG - 1, (NG - 1) % 2, more=False)
            phase2(NG, NG % 2, a=False)
            phase2(NG + 1, (NG + 1) % 2, a=False, b=False)

        @block.gpsimd
        def _(pool):
            ptt, pts = pool.tensor_tensor, pool.tensor_scalar

            def rstd(which, mvs, count, done, plus_one=None):
                need(pool, mvs, count)
                ptt(veps[which][:], mv[which][:, :, 1], eps[:], ALU.add)
                pts(nmean[which][:], mv[which][:, :, 0], -1.0, None, ALU.mult)
                pool.drain()
                ptt(rs[which][:], veps[which][:], neg_half[:], ALU.pow)
                pool.drain()
                if plus_one is not None:
                    pts(plus_one[:], rs[which][:], 1.0, None, ALU.add)
                ptt(nm[which][:], nmean[which][:], rs[which][:], ALU.mult).then_inc(sem(done), 1)

            pool.memset(ident[:], 0.0)
            pool.memset(neg_half[:], -0.5)
            pool.memset(eps[:], LN_EPS)
            pool.drain()
            pool.affine_select(out=ident[:], in_=ident[:], compare_op=ALU.not_equal, fill=1.0, base=0,
                               pattern=[[-1, P]], channel_multiplier=1).then_inc(sem("ident"), 1)
            rstd(LX[0], "mv_x1", 1, "rs_x1")
            pool.memset(ew2_raw, 0.0)
            pool.memset(out_bias[:].bitcast(F32), 0.0).then_inc(sem("zeroed"), 1)
            for n in range(2):
                pool.memset(xr_hi[n][:, :, C:C + 1].bitcast(F32), 1.0)
                pool.memset(xr_hi[n][:, :, C + 1:C + 2].bitcast(F32), 0.0)
                last = pool.memset(xr_lo[n][:, :, C:C + 2].bitcast(F32), 0.0)
            last.then_inc(sem("xr_ones"), 1)

            def p1_rstd(v, par):
                need(pool, "xn1", T * (v - 1))
                rstd(LX[par], "mv_x1", v + 1, "rs_x1")

            def phase1(v, par, more=True):
                if more:
                    p1_rstd(v + 2, par)
                need(pool, "xr_hi", v + 1)
                need(pool, "kx", v - 1)
                ptt(xr_lo[par][:, :, 0:C], xn1[par][:], xr_hi[par][:, :, 0:C], ALU.subtract).then_inc(sem("x_split"), 1)
                need(pool, "k_hi", v + 1)
                ptt(k_lo[par][:], kf[:], k_hi[par][:], ALU.subtract).then_inc(sem("k_split"), 1)

            p1_rstd(1, 1)
            phase1(0, 0)
            pool.memset(beats[:], 1.0)
            pool.memset(scale_rows[:], 0.0)
            pool.drain()
            for at in (0, 64):
                pool.memset(scale_rows[:, :, at + EXPERTS:at + EXPERTS + 1], 1.0)
            for n, sign in ((0, 1), (1, -1)):
                last = pool.affine_select(out=beats[:, :, n, :], in_=beats[:, :, n, :], compare_op=ALU.is_gt, fill=0.0,
                                          base=0, pattern=[[sign, EXPERTS], [-sign, EXPERTS]], channel_multiplier=0)
            last.then_inc(sem("masks"), 1)
            phase1(1, 1)
            steps(pool, phase1, 2, NG - 3)

            def rs_of_x(v, par):
                need(pool, f"idx{par}", 2 * dma16(v, par))
                need(pool, "t", v - 1)
                need(pool, "gnn", v - 1)
                rstd(LX[par], "mv_x", v + 1, "rs_x", plus_one=rs1[par])

            for v in range(NG - 3, NG):
                if v == NG - 1:
                    need(pool, "xn1", T * NG)
                    rs_of_x(0, 0)
                phase1(v, v % 2, more=v + 2 < NG)
            pool.drain().then_inc(sem("p1_pool"), 1)

            def gathers(par):
                for j in range(T):
                    pool.indirect_dma_start(xg[par][:, j, :], None, table_xt.ap(), bass.IndirectOffsetOnAxis(
                        idx[par][:, 1, j:j + 1], 0)).then_inc(sem("gath"), 16)
                    pool.indirect_dma_start(ag[par][:, j, :], None, table_al.ap(), bass.IndirectOffsetOnAxis(
                        idx[par][:, 0, j:j + 1], 0)).then_inc(sem("gath"), 16)

            def low(out, src, hi, done):
                ptt(out, src, hi, ALU.subtract).then_inc(sem(done), 1)

            def phase2(i, par, a=True, b=True, c=True, more=True):
                if a:
                    gathers(par)
                if b:
                    for n in range(2):
                        need(pool, "h_relu", 4 * (i - 1) + 2 * n + 2)
                        low(h_lo[:, 2 * n:2 * n + 2, :], relu[n][:], h_hi[:, 2 * n:2 * n + 2, :], "h_lo")
                if c:
                    need(pool, "s1_relu", 2 * (i - 1))
                    low(s1_lo[:], relu[2][:], s1_hi[:], "s1_lo")
                if b:
                    need(pool, "t", i)
                    need(pool, "gnn", i)
                    bv = base[:].rearrange("p j (h d) -> p j h d", h=HEADS)
                    ptt(bv, bv, gnn[:].unsqueeze(2).broadcast_to([R, T, HEADS, HEAD_CH]),
                        ALU.add).then_inc(sem("base"), 1)
                if c:
                    for n in range(2):
                        need(pool, "e1_relu", 4 * (i - 2) + 2 * n + 2)
                        low(e1_lo[:, 2 * n:2 * n + 2, :], relu[n][:], e1_hi[:, 2 * n:2 * n + 2, :], "e1_lo")
                if a and more:
                    rs_of_x(i + 1, 1 - par)
                if b:
                    need(pool, "y", i - 1)
                    rstd(LY, "mv_y", i, "rs_y")
                if c:
                    need(pool, "s2_relu", i - 1)
                    low(s2_lo[:], relu[2][:, 0, :], s2_hi[:], "s2_lo")
                if a:
                    need(pool, "m_norm", T * i)
                    rstd(LM, "mv_m", i + 1, "rs_m")
                if b:
                    need(pool, "z_norm", T * (i - 1))
                    rstd(LZ, "mv_z", i, "rs_z")

            enter_phase2(pool)
            phase2(0, 0, b=False, c=False)
            phase2(1, 1, c=False)
            phase2(2, 0)
            steps(pool, phase2, 3, NG - 1)
            phase2(NG - 1, (NG - 1) % 2, more=False)
            phase2(NG, NG % 2, a=False)
            phase2(NG + 1, (NG + 1) % 2, a=False, b=False)


_INS = ["x", "src", "dst", "L0_gnn_weight", "L0_gnn_attn_l", "L0_gnn_attn_r", "L0_mix_Wq", "L0_mix_Wk", "L0_mix_Wv",
        "L0_mix_Wm", "L0_mix_W1", "L0_mix_W2", "L0_mix_g1", "L0_mix_b1", "L0_mix_g2", "L0_mix_b2", "L0_ffn_sW1",
        "L0_ffn_sb1", "L0_ffn_sW2", "L0_ffn_sb2", "L0_ffn_sW3", "L0_ffn_sb3", "L0_ffn_eW1", "L0_ffn_eb1",
        "L0_ffn_eW2", "L0_ffn_eb2", "L0_ffn_eW3", "L0_ffn_eb3", "L0_ffn_gW", "L0_ffn_gb"]


def kernel(**inputs):
    import numpy as np
    import concourse.bacc as bacc
    from concourse.bass_utils import run_bass_kernel_spmd

    nc = bacc.Bacc("TRN2", target_bir_lowering=False, num_devices=1)
    arrays, aps = {}, {}
    for name in _INS:
        a = np.ascontiguousarray(inputs[name])
        arrays[f"in_{name}"] = a
        aps[name] = nc.dram_tensor(f"in_{name}", a.shape, mybir.dt.from_np(a.dtype), kind="ExternalInput").ap()
    aps["out"] = nc.dram_tensor("out_0", (N_NODES, C), F32, kind="ExternalOutput").ap()
    gps_layer(nc, aps)
    r = run_bass_kernel_spmd(nc, [arrays], core_ids=[0])
    return r.results[0]["out_0"]
```
